# Optimizing a Trainium2 kernel written in Bass

```python
import numpy as np
import jax
import jax.numpy as jnp

def _softmax(x, axis=-1):
    return jax.nn.softmax(x, axis=axis)

def _gelu(x):
    return jax.nn.gelu(x, approximate=True)

def _silu(x):
    return jax.nn.silu(x)

def _sigmoid(x):
    return jax.nn.sigmoid(x)

def _layernorm(x, axis=-1, eps=1e-05):
    m = jnp.mean(x, axis=axis, keepdims=True)
    v = jnp.var(x, axis=axis, keepdims=True)
    return (x - m) / jnp.sqrt(v + eps)

def _scatter_add(tgt, idx, src, axis=0):
    return tgt.at[idx].add(src)

def _segment_sum(src, seg, n):
    return jax.ops.segment_sum(src, seg, n)
kernel_name = 'mk_flamingo_gated_d2_seqx_r8_93abd3'

def setup_inputs(seed: int=0):
    np.random.seed(seed)
    _w = jnp.asarray

    def _rec_inputs():
        import jax
        import jax.numpy as jnp
        _rk = jax.random.key(seed)
        x = 7.22e-05 + 1 * jax.random.normal(jax.random.fold_in(_rk, 1), (16, 100, 256), jnp.float32)
        _lenS = 100 - jax.random.randint(jax.random.fold_in(_rk, 7), (16,), 0, max(1, 100 // 4) + 1, jnp.int32)
        _lenS2 = 1444 - jax.random.randint(jax.random.fold_in(_rk, 8), (16,), 0, max(1, 1444 // 4) + 1, jnp.int32)
        _ctx_512P = jax.random.normal(jax.random.fold_in(_rk, 11), (16, 16, 64), jnp.float32)
        _ctx_512c = jax.random.dirichlet(jax.random.fold_in(_rk, 511), 0.3 * jnp.ones((16,), jnp.float32), (16, 1444))
        _ctx_512t = jnp.einsum('bsk,bkd->bsd', _ctx_512c, _ctx_512P)
        _ctx_512t = _ctx_512t * jax.lax.rsqrt(jnp.mean(jnp.square(_ctx_512t)) + 1e-12) * 0.953939
        ctx_512 = -0.000514642 + 1.00011 * (_ctx_512t + 0.3 * jax.random.normal(jax.random.fold_in(_rk, 611), (16, 1444, 64), jnp.float32))
        _g = jax.random.normal(jax.random.fold_in(_rk, 9001), (2, 2), jnp.float32)
        _g = jnp.sign(_g) * jnp.maximum(jnp.abs(_g), 1.0) + (_g == 0) * 1.0
        g_xattn = _g[0]
        g_ffn = _g[1]
        return (x, ctx_512, g_xattn, g_ffn)
    x, ctx_512, g_xattn, g_ffn = _rec_inputs()

    def _L0_xattn_setup():
        import jax, jax.numpy as jnp
        import numpy as np
        B, S, H, NH, L = (2, 256, 256, 16, 64)
        HD = H // NH
        key = jax.random.key(seed)
        k1, k2, k3, k4, k5 = jax.random.split(key, 5)
        scale = 0.02
        return {'q': jax.random.normal(k1, (B, S, H), dtype=jnp.float32), 'latent_kv': jax.random.normal(k2, (B, S, L), dtype=jnp.float32), 'Wq': jax.random.normal(k3, (H, H), dtype=jnp.float32) * scale, 'Wkv_expand': jax.random.normal(k4, (2 * H, L), dtype=jnp.float32) * scale, 'Wout': jax.random.normal(k5, (H, H), dtype=jnp.float32) * scale}
    _L0_xattn_all = _L0_xattn_setup()
    _L0_xattn_in = {k: v for k, v in _L0_xattn_all.items() if k in ('Wq', 'Wkv_expand', 'Wout')}
    del _L0_xattn_all

    def _L0_ffn_setup():
        import jax, jax.numpy as jnp
        import numpy as np
        B, S, H = (2, 256, 256)
        E, G, TKG, K = (32, 8, 4, 8)
        I, SI = (128, 256)
        ROUTED_SCALE = 2.5

        def _moe_forward(hidden_states, router_w, router_bias, w_gate, w_up, w_down, sw_gate, sw_up, sw_down):
            x = hidden_states.reshape(-1, H)
            T = x.shape[0]
            logits = x.astype(jnp.float32) @ router_w.astype(jnp.float32)
            scores = jax.nn.sigmoid(logits)
            scores_grouped = (scores + router_bias).reshape(T, G, E // G)
            top2, _ = jax.lax.top_k(scores_grouped, 2)
            group_scores = top2.sum(-1)
            _, top_groups = jax.lax.top_k(group_scores, TKG)
            mask = jnp.ones((T, G), bool).at[jnp.arange(T)[:, None], top_groups].set(False)
            masked = jnp.where(mask[:, :, None], 0.0, scores_grouped).reshape(T, E)
            _, top_k_index = jax.lax.top_k(masked, K)
            tkw = jnp.take_along_axis(scores, top_k_index, axis=-1)
            tkw = tkw / tkw.sum(-1, keepdims=True)
            tkw = (tkw * ROUTED_SCALE).astype(hidden_states.dtype)
            flat_idx = top_k_index.reshape(-1)
            sort_idx = jnp.argsort(flat_idx)
            xs = jnp.repeat(x, K, axis=0)[sort_idx]
            group_sizes = jnp.bincount(flat_idx, length=E).astype(jnp.int32)
            gate = jax.lax.ragged_dot(xs, w_gate, group_sizes)
            up = jax.lax.ragged_dot(xs, w_up, group_sizes)
            down = jax.lax.ragged_dot(jax.nn.silu(gate) * up, w_down, group_sizes)
            unsort = jnp.argsort(sort_idx)
            routed = (down[unsort].reshape(T, K, H) * tkw[..., None]).sum(axis=1)
            shared = jax.nn.silu(x @ sw_gate) * (x @ sw_up) @ sw_down
            return (routed + shared).reshape(hidden_states.shape)
        key = jax.random.key(seed)
        ks = jax.random.split(key, 9)

        def w(k, shape, fan_in):
            return jax.random.normal(k, shape, jnp.float32) / np.float32(np.sqrt(fan_in))
        return dict(hidden_states=jax.random.normal(ks[0], (B, S, H), jnp.float32), router_w=w(ks[1], (H, E), H), router_bias=jnp.zeros((E,), jnp.float32), w_gate=w(ks[2], (E, H, I), H), w_up=w(ks[3], (E, H, I), H), w_down=w(ks[4], (E, I, H), I), sw_gate=w(ks[5], (H, SI), H), sw_up=w(ks[6], (H, SI), H), sw_down=w(ks[7], (SI, H), SI))
    _L0_ffn_all = _L0_ffn_setup()
    _L0_ffn_in = {k: v for k, v in _L0_ffn_all.items() if k in ('router_w', 'router_bias', 'w_gate', 'w_up', 'w_down', 'sw_gate', 'sw_up', 'sw_down')}
    del _L0_ffn_all

    def _L1_xattn_setup():
        import jax, jax.numpy as jnp
        import numpy as np
        B, S, L = (2, 128, 128)
        DIM_Q, H, K, D_C, D_CQ, R = (256, 16, 128, 64, 192, 64)

        def _rope_tables(length, dim):
            inv = 1.0 / 10000.0 ** (jnp.arange(0, dim, 2, dtype=jnp.float32) / dim)
            f = jnp.arange(length, dtype=jnp.float32)[:, None] * inv[None, :]
            sin = jnp.repeat(jnp.sin(f), 2, axis=-1)
            cos = jnp.repeat(jnp.cos(f), 2, axis=-1)
            return (sin, cos)

        def _rotate_half(x):
            half = x.shape[-1] // 2
            return jnp.concatenate([-x[..., half:], x[..., :half]], axis=-1)

        def _apply_rope(x, sin, cos):
            return x * cos + _rotate_half(x) * sin
        key = jax.random.key(seed)
        ks = jax.random.split(key, 8)
        return {'hidden_q': jax.random.normal(ks[0], (B, S, DIM_Q), jnp.float32), 'kv_c': jax.random.normal(ks[1], (B, L, D_C), jnp.float32), 'Wq': jax.random.normal(ks[2], (H * K, DIM_Q), jnp.float32) / np.sqrt(DIM_Q).astype(np.float32), 'w_kc_q': jax.random.normal(ks[3], (H, K, D_CQ), jnp.float32) / np.sqrt(K).astype(np.float32), 'w_kc_kv': jax.random.normal(ks[4], (H, K, D_C), jnp.float32) / np.sqrt(K).astype(np.float32), 'W_qr': jax.random.normal(ks[5], (H, D_CQ, R), jnp.float32) / np.float32(np.sqrt(D_CQ) * np.sqrt(R)), 'W_kr': jax.random.normal(ks[6], (H, D_C, R), jnp.float32) / np.sqrt(D_C).astype(np.float32), 'Wo': jax.random.normal(ks[7], (DIM_Q, H * K), jnp.float32) / np.sqrt(H * K).astype(np.float32)}
    _L1_xattn_all = _L1_xattn_setup()
    _L1_xattn_in = {k: v for k, v in _L1_xattn_all.items() if k in ('Wq', 'w_kc_q', 'w_kc_kv', 'W_qr', 'W_kr', 'Wo')}
    del _L1_xattn_all

    def _L1_ffn_setup():
        import jax, jax.numpy as jnp
        import numpy as np
        N_EXPERTS = 16
        TOP_K = 4
        N_GROUP = 4
        TOPK_GROUP = 2
        NORM_TOPK = True
        ROUTED_SCALE = 2.5
        H = 256
        F_MOE = 128
        F_SHARED = 256
        B, S = (2, 256)

        def _route(hidden, gate_weight, bias):
            T = hidden.shape[0]
            epg = N_EXPERTS // N_GROUP
            logits = hidden @ gate_weight.T
            scores = jax.nn.sigmoid(logits)
            scores_for_choice = scores + bias[None, :]
            grp = scores_for_choice.reshape(T, N_GROUP, epg)
            group_scores = jax.lax.top_k(grp, 2)[0].sum(-1)
            group_idx = jax.lax.top_k(group_scores, TOPK_GROUP)[1]
            group_mask = jax.nn.one_hot(group_idx, N_GROUP, dtype=jnp.bool_).any(1)
            score_mask = jnp.repeat(group_mask, epg, axis=-1)
            masked = jnp.where(score_mask, scores_for_choice, -jnp.inf)
            topk_idx = jax.lax.top_k(masked, TOP_K)[1]
            topk_weight = jnp.take_along_axis(scores, topk_idx, axis=1)
            return (topk_weight, topk_idx)

        def _swiglu(x, gw, uw, dw):
            return jax.nn.silu(x @ gw.T) * (x @ uw.T) @ dw.T
        key = jax.random.key(seed)
        ks = jax.random.split(key, 9)
        std = 0.02
        return {'hidden_states': jax.random.normal(ks[0], (B, S, H), jnp.float32), 'gate_weight': jax.random.normal(ks[1], (N_EXPERTS, H), jnp.float32) * std, 'e_score_correction_bias': jnp.zeros((N_EXPERTS,), jnp.float32), 'gate_w': jax.random.normal(ks[2], (N_EXPERTS, F_MOE, H), jnp.float32) * std, 'up_w': jax.random.normal(ks[3], (N_EXPERTS, F_MOE, H), jnp.float32) * std, 'down_w': jax.random.normal(ks[4], (N_EXPERTS, H, F_MOE), jnp.float32) * std, 'sh_gate_w': jax.random.normal(ks[5], (F_SHARED, H), jnp.float32) * std, 'sh_up_w': jax.random.normal(ks[6], (F_SHARED, H), jnp.float32) * std, 'sh_down_w': jax.random.normal(ks[7], (H, F_SHARED), jnp.float32) * std}
    _L1_ffn_all = _L1_ffn_setup()
    _L1_ffn_in = {k: v for k, v in _L1_ffn_all.items() if k in ('gate_weight', 'e_score_correction_bias', 'gate_w', 'up_w', 'down_w', 'sh_gate_w', 'sh_up_w', 'sh_down_w')}
    del _L1_ffn_all
    return {'x': x, 'ctx_512': ctx_512, 'g_xattn': g_xattn, 'g_ffn': g_ffn, 'L0_xattn_Wq': _L0_xattn_in['Wq'], 'L0_xattn_Wkv_expand': _L0_xattn_in['Wkv_expand'], 'L0_xattn_Wout': _L0_xattn_in['Wout'], 'L0_ffn_router_w': _L0_ffn_in['router_w'], 'L0_ffn_router_bias': _L0_ffn_in['router_bias'], 'L0_ffn_w_gate': _L0_ffn_in['w_gate'], 'L0_ffn_w_up': _L0_ffn_in['w_up'], 'L0_ffn_w_down': _L0_ffn_in['w_down'], 'L0_ffn_sw_gate': _L0_ffn_in['sw_gate'], 'L0_ffn_sw_up': _L0_ffn_in['sw_up'], 'L0_ffn_sw_down': _L0_ffn_in['sw_down'], 'L1_xattn_Wq': _L1_xattn_in['Wq'], 'L1_xattn_w_kc_q': _L1_xattn_in['w_kc_q'], 'L1_xattn_w_kc_kv': _L1_xattn_in['w_kc_kv'], 'L1_xattn_W_qr': _L1_xattn_in['W_qr'], 'L1_xattn_W_kr': _L1_xattn_in['W_kr'], 'L1_xattn_Wo': _L1_xattn_in['Wo'], 'L1_ffn_gate_weight': _L1_ffn_in['gate_weight'], 'L1_ffn_e_score_correction_bias': _L1_ffn_in['e_score_correction_bias'], 'L1_ffn_gate_w': _L1_ffn_in['gate_w'], 'L1_ffn_up_w': _L1_ffn_in['up_w'], 'L1_ffn_down_w': _L1_ffn_in['down_w'], 'L1_ffn_sh_gate_w': _L1_ffn_in['sh_gate_w'], 'L1_ffn_sh_up_w': _L1_ffn_in['sh_up_w'], 'L1_ffn_sh_down_w': _L1_ffn_in['sh_down_w']}

def reference(x, ctx_512, g_xattn, g_ffn, L0_xattn_Wq, L0_xattn_Wkv_expand, L0_xattn_Wout, L0_ffn_router_w, L0_ffn_router_bias, L0_ffn_w_gate, L0_ffn_w_up, L0_ffn_w_down, L0_ffn_sw_gate, L0_ffn_sw_up, L0_ffn_sw_down, L1_xattn_Wq, L1_xattn_w_kc_q, L1_xattn_w_kc_kv, L1_xattn_W_qr, L1_xattn_W_kr, L1_xattn_Wo, L1_ffn_gate_weight, L1_ffn_e_score_correction_bias, L1_ffn_gate_w, L1_ffn_up_w, L1_ffn_down_w, L1_ffn_sh_gate_w, L1_ffn_sh_up_w, L1_ffn_sh_down_w):
    import jax
    import jax.numpy as jnp

    def _L0_xattn_ref(q, latent_kv, Wq, Wkv_expand, Wout):
        import jax, jax.numpy as jnp
        import numpy as np
        B, S, H, NH, L = (2, 256, 256, 16, 64)
        HD = H // NH
        b, sq, _ = q.shape
        sk = latent_kv.shape[1]
        qp = q @ Wq.T
        kv = latent_kv @ Wkv_expand.T
        k, v = jnp.split(kv, 2, axis=-1)
        qh = qp.reshape(b, sq, NH, HD).transpose(0, 2, 1, 3)
        kh = k.reshape(b, sk, NH, HD).transpose(0, 2, 1, 3)
        vh = v.reshape(b, sk, NH, HD).transpose(0, 2, 1, 3)
        inv_sqrt_d = 1.0 / jnp.sqrt(jnp.float32(HD))
        scores = jnp.einsum('bhqd,bhkd->bhqk', qh, kh) * inv_sqrt_d
        causal = jnp.tril(jnp.ones((sq, sk), dtype=bool))
        scores = jnp.where(causal, scores, jnp.finfo(scores.dtype).min)
        attn = jax.nn.softmax(scores, axis=-1)
        out = jnp.einsum('bhqk,bhkd->bhqd', attn, vh)
        out = out.transpose(0, 2, 1, 3).reshape(b, sq, H)
        return out @ Wout.T

    def _L0_ffn_ref(hidden_states, router_w, router_bias, w_gate, w_up, w_down, sw_gate, sw_up, sw_down):
        import jax, jax.numpy as jnp
        import numpy as np
        B, S, H = (2, 256, 256)
        E, G, TKG, K = (32, 8, 4, 8)
        I, SI = (128, 256)
        ROUTED_SCALE = 2.5

        def _moe_forward(hidden_states, router_w, router_bias, w_gate, w_up, w_down, sw_gate, sw_up, sw_down):
            x = hidden_states.reshape(-1, H)
            T = x.shape[0]
            logits = x.astype(jnp.float32) @ router_w.astype(jnp.float32)
            scores = jax.nn.sigmoid(logits)
            scores_grouped = (scores + router_bias).reshape(T, G, E // G)
            top2, _ = jax.lax.top_k(scores_grouped, 2)
            group_scores = top2.sum(-1)
            _, top_groups = jax.lax.top_k(group_scores, TKG)
            mask = jnp.ones((T, G), bool).at[jnp.arange(T)[:, None], top_groups].set(False)
            masked = jnp.where(mask[:, :, None], 0.0, scores_grouped).reshape(T, E)
            _, top_k_index = jax.lax.top_k(masked, K)
            tkw = jnp.take_along_axis(scores, top_k_index, axis=-1)
            tkw = tkw / tkw.sum(-1, keepdims=True)
            tkw = (tkw * ROUTED_SCALE).astype(hidden_states.dtype)
            flat_idx = top_k_index.reshape(-1)
            sort_idx = jnp.argsort(flat_idx)
            xs = jnp.repeat(x, K, axis=0)[sort_idx]
            group_sizes = jnp.bincount(flat_idx, length=E).astype(jnp.int32)
            gate = jax.lax.ragged_dot(xs, w_gate, group_sizes)
            up = jax.lax.ragged_dot(xs, w_up, group_sizes)
            down = jax.lax.ragged_dot(jax.nn.silu(gate) * up, w_down, group_sizes)
            unsort = jnp.argsort(sort_idx)
            routed = (down[unsort].reshape(T, K, H) * tkw[..., None]).sum(axis=1)
            shared = jax.nn.silu(x @ sw_gate) * (x @ sw_up) @ sw_down
            return (routed + shared).reshape(hidden_states.shape)
        return _moe_forward(hidden_states, router_w, router_bias, w_gate, w_up, w_down, sw_gate, sw_up, sw_down)

    def _L1_xattn_ref(hidden_q, kv_c, Wq, w_kc_q, w_kc_kv, W_qr, W_kr, Wo):
        import jax, jax.numpy as jnp
        import numpy as np
        B, S, L = (2, 128, 128)
        DIM_Q, H, K, D_C, D_CQ, R = (256, 16, 128, 64, 192, 64)

        def _rope_tables(length, dim):
            inv = 1.0 / 10000.0 ** (jnp.arange(0, dim, 2, dtype=jnp.float32) / dim)
            f = jnp.arange(length, dtype=jnp.float32)[:, None] * inv[None, :]
            sin = jnp.repeat(jnp.sin(f), 2, axis=-1)
            cos = jnp.repeat(jnp.cos(f), 2, axis=-1)
            return (sin, cos)

        def _rotate_half(x):
            half = x.shape[-1] // 2
            return jnp.concatenate([-x[..., half:], x[..., :half]], axis=-1)

        def _apply_rope(x, sin, cos):
            return x * cos + _rotate_half(x) * sin
        Bv, Sv, _ = hidden_q.shape
        _, Lv, _ = kv_c.shape
        q_hk = (hidden_q @ Wq.T).reshape(Bv, Sv, H, K)
        q_big = jnp.einsum('bshk,hkq->bshq', q_hk, w_kc_q)
        sin_q, cos_q = _rope_tables(Sv, D_CQ)
        q_big = _apply_rope(q_big, sin_q[None, :, None, :], cos_q[None, :, None, :])
        sin_k, cos_k = _rope_tables(Lv, D_C)
        kv_r = _apply_rope(kv_c, sin_k[None], cos_k[None])
        q_r = jnp.einsum('bshq,hqr->bhsr', q_big, W_qr)
        k_r = jnp.einsum('bld,hdr->bhlr', kv_r, W_kr)
        scores = jnp.einsum('bhsr,bhlr->bhsl', q_r, k_r)
        attn = jax.nn.softmax(scores, axis=-1)
        ctx_c = jnp.einsum('bhsl,bld->bhsd', attn, kv_r)
        ctx_lat = jnp.einsum('bhsd,hkd->bhsk', ctx_c, w_kc_kv)
        ctx = ctx_lat.transpose(0, 2, 1, 3).reshape(Bv, Sv, H * K)
        return ctx @ Wo.T

    def _L1_ffn_ref(hidden_states, gate_weight, e_score_correction_bias, gate_w, up_w, down_w, sh_gate_w, sh_up_w, sh_down_w):
        import jax, jax.numpy as jnp
        import numpy as np
        N_EXPERTS = 16
        TOP_K = 4
        N_GROUP = 4
        TOPK_GROUP = 2
        NORM_TOPK = True
        ROUTED_SCALE = 2.5
        H = 256
        F_MOE = 128
        F_SHARED = 256
        B, S = (2, 256)

        def _route(hidden, gate_weight, bias):
            T = hidden.shape[0]
            epg = N_EXPERTS // N_GROUP
            logits = hidden @ gate_weight.T
            scores = jax.nn.sigmoid(logits)
            scores_for_choice = scores + bias[None, :]
            grp = scores_for_choice.reshape(T, N_GROUP, epg)
            group_scores = jax.lax.top_k(grp, 2)[0].sum(-1)
            group_idx = jax.lax.top_k(group_scores, TOPK_GROUP)[1]
            group_mask = jax.nn.one_hot(group_idx, N_GROUP, dtype=jnp.bool_).any(1)
            score_mask = jnp.repeat(group_mask, epg, axis=-1)
            masked = jnp.where(score_mask, scores_for_choice, -jnp.inf)
            topk_idx = jax.lax.top_k(masked, TOP_K)[1]
            topk_weight = jnp.take_along_axis(scores, topk_idx, axis=1)
            return (topk_weight, topk_idx)

        def _swiglu(x, gw, uw, dw):
            return jax.nn.silu(x @ gw.T) * (x @ uw.T) @ dw.T
        Bh, Sh, Hh = hidden_states.shape
        hidden = hidden_states.reshape(-1, Hh)
        topk_weight, topk_idx = _route(hidden, gate_weight, e_score_correction_bias)
        if NORM_TOPK:
            topk_weight = topk_weight / (topk_weight.sum(-1, keepdims=True) + 1e-20)
        topk_weight = topk_weight * ROUTED_SCALE
        one_hot = jax.nn.one_hot(topk_idx, N_EXPERTS, dtype=topk_weight.dtype)
        weight_matrix = (one_hot * topk_weight[..., None]).sum(1)
        g = jnp.einsum('th,nfh->ntf', hidden, gate_w)
        u = jnp.einsum('th,nfh->ntf', hidden, up_w)
        act = jax.nn.silu(g) * u
        routed = jnp.einsum('ntf,nhf,tn->th', act, down_w, weight_matrix)
        out = routed + _swiglu(hidden, sh_gate_w, sh_up_w, sh_down_w)
        return out.reshape(Bh, Sh, Hh)
    x = x + jnp.tanh(g_xattn[0]) * _L0_xattn_ref(_layernorm(x, axis=-1), ctx_512, L0_xattn_Wq, L0_xattn_Wkv_expand, L0_xattn_Wout)
    x = x + jnp.tanh(g_ffn[0]) * _L0_ffn_ref(_layernorm(x, axis=-1), L0_ffn_router_w, L0_ffn_router_bias, L0_ffn_w_gate, L0_ffn_w_up, L0_ffn_w_down, L0_ffn_sw_gate, L0_ffn_sw_up, L0_ffn_sw_down)
    x = x + jnp.tanh(g_xattn[1]) * _L1_xattn_ref(_layernorm(x, axis=-1), ctx_512, L1_xattn_Wq, L1_xattn_w_kc_q, L1_xattn_w_kc_kv, L1_xattn_W_qr, L1_xattn_W_kr, L1_xattn_Wo)
    x = x + jnp.tanh(g_ffn[1]) * _L1_ffn_ref(_layernorm(x, axis=-1), L1_ffn_gate_weight, L1_ffn_e_score_correction_bias, L1_ffn_gate_w, L1_ffn_up_w, L1_ffn_down_w, L1_ffn_sh_gate_w, L1_ffn_sh_up_w, L1_ffn_sh_down_w)
    return x

_drawn_inputs = setup_inputs


def setup_inputs(seed=0):
    import zlib

    import numpy as np

    out = dict(_drawn_inputs(seed))
    spreads = {'g_ffn': (-1.0, 0.6),
     'L0_ffn_router_bias': (0.0, 0.1),
     'L1_ffn_e_score_correction_bias': (0.0, 0.779)}
    factors = {'L0_xattn_Wq': 7.393,
     'L1_ffn_gate_weight': 7.816,
     'L1_ffn_gate_w': 5.445,
     'L1_ffn_up_w': 5.394,
     'L1_ffn_down_w': 5.369,
     'L1_ffn_sh_gate_w': 4.875,
     'L1_ffn_sh_up_w': 4.819,
     'L1_ffn_sh_down_w': 4.826}
    for name, (base, spread) in spreads.items():
        noise = np.random.default_rng([zlib.crc32(name.encode()), seed]).standard_normal(out[name].shape)
        drawn = base * np.exp(spread * noise) if base else spread * noise
        out[name] = jnp.asarray(drawn.astype(out[name].dtype))
    for name, factor in factors.items():
        out[name] = (out[name] * factor).astype(out[name].dtype)
    return out
```

```python
from contextlib import ExitStack
import math

import concourse.bass as bass
from concourse import mybir
import numpy as np

F32 = mybir.dt.float32
F32R = mybir.dt.float32r
BF16 = mybir.dt.bfloat16
ALU = mybir.AluOpType
ACT = mybir.ActivationFunctionType
AX = mybir.AxisListType

NB, SQ, D = 16, 100, 256
T = NB * SQ
NH = 16
SK, DC = 1444, 64
KT = D // 128
NKT = (SK + 127) // 128
KREST = SK - (NKT - 1) * 128
HQ = NH * SQ
CH = 4 * SQ
NCH = HQ // CH
DCQ, HALF = 192, 96
FF = 128
EPS = 1e-5
LN2 = math.log(2)
LOWEST = -3.0e38
HIGHEST, CHOSEN = 3.0e38, 2.0e38


def ds(start, n):
    return bass.ds(start, n)


class Core:

    def __init__(self, nc, dram, stack):
        self.nc, self.dram, self.stack = nc, dram, stack
        self.used = []
        self.psum = stack.enter_context(nc.psum_tensor("psum", [128, 8, 512], F32))
        self.x = self.sbuf("x_sb", [SQ, NB, D], F32)
        self.xnH = self.sbuf("xnH", [128, KT, T], F32R)
        self.xnL = self.sbuf("xnL", [128, KT, T], F32R)
        self.ident = self.sbuf("ident", [128, 128], F32)
        self.gates = self.sbuf("gates", [128, 4], F32)

    def sbuf(self, name, shape, dtype, stack=None):
        return (stack or self.stack).enter_context(self.nc.sbuf_tensor(name, shape, dtype))

    def sem(self, stack, name):
        handle = stack.enter_context(self.nc.semaphore(name))
        self.used.append(handle.num)
        return handle

    def clear_semaphores(self):
        with self.nc.Block() as block:
            @block.sync
            def _(sp):
                sp.sem_clear(range(min(self.used), max(self.used) + 1))
        self.used = []



def prepare_0(k, wa, v0, maskq, identb):
    nc, P = k.nc, k.psum
    waH, waL = wa
    with ExitStack() as st:
        w = k.sbuf("w_attn0", [16, NH, 640], F32, st)
        graw = k.sbuf("graw", [128, 4], F32, st)
        loaded = k.sem(st, "p0_loaded")
        qk_done, vo_done, high_done, low_done = (k.sem(st, f"p0_{n}") for n in ("qk", "vo", "high", "low"))
        with nc.Block() as block:
            @block.sync
            def _(sp):
                sp.dma_start(w[:], k.dram["w_attn0"]).then_inc(loaded, 16)
                sp.dma_start(k.ident[:], k.dram["ident"]).then_inc(loaded, 16)
                sp.dma_start(graw[:, 0:2], k.dram["g_xattn"].partition_broadcast(128)).then_inc(loaded, 16)
                sp.dma_start(graw[:, 2:4], k.dram["g_ffn"].partition_broadcast(128)).then_inc(loaded, 16)
                sp.dma_start(maskq[:], k.dram["mask"]).then_inc(loaded, 16)
                sp.dma_start(identb[:], k.dram["ident_bf16"]).then_inc(loaded, 16)
                sp.dma_start(k.x[:], k.dram["x"].rearrange("b q d -> q b d")).then_inc(loaded, 16)

            @block.tensor
            def _(pe):
                pe.wait_ge(loaded, 112)
                for h in range(NH):
                    for kt in range(KT):
                        last = nc.tensor.matmul(P[:, 2 * kt + h % 8 // 4, (2 * (h % 4) + h // 8) * DC:(2 * (h % 4) + h // 8 + 1) * DC],
                                                w[:, h, kt * 128:(kt + 1) * 128], w[:, h, 256:320],
                                                start=True, stop=True)
                last.then_inc(qk_done, 1)
                for h in range(NH):
                    pair, up = 4 * (h // 8) + h % 4, (h // 4) % 2
                    last = nc.tensor.matmul(P[64 * up:64 * up + 64, 4 + pair // 2, (pair % 2) * D:(pair % 2 + 1) * D],
                                            w[:, h, 320:384], w[:, h, 384:640], start=True, stop=True)
                last.then_inc(vo_done, 1)

            @block.scalar
            def _(act):
                act.wait_ge(loaded, 112)
                nc.scalar.activation(k.gates[:], graw[:], ACT.Tanh)
                act.wait_ge(qk_done, 1)
                nc.scalar.activation(waH[:].rearrange("p t n -> p (t n)"),
                                     P[:, 0:4, :].rearrange("p b n -> p (b n)"), ACT.Copy, scale=0.25).then_inc(high_done, 1)
                act.wait_ge(vo_done, 1)
                nc.scalar.copy(v0[:].rearrange("p t n -> p (t n)"), P[:, 4:8, :].rearrange("p b n -> p (b n)"))

            @block.vector
            def _(dve):
                dve.wait_ge(high_done, 1)
                nc.vector.scalar_tensor_tensor(out=waL[:].rearrange("p t n -> p (t n)"),
                                               in0=P[:, 0:4, :].rearrange("p b n -> p (b n)"), scalar=0.25,
                                               in1=waH[:].rearrange("p t n -> p (t n)").bitcast(F32),
                                               op0=ALU.mult, op1=ALU.subtract).then_inc(low_done, 1)



def layer_norm(k, tag):
    nc, P = k.nc, k.psum
    GRP = 2
    with ExitStack() as st:
        stats = k.sbuf(f"ln_stats{tag}", [SQ, NB, 6], F32, st)
        mv = k.sbuf(f"ln_mv{tag}", [SQ, NB, 2], F32, st)
        std = k.sbuf(f"ln_std{tag}", [SQ, NB], F32, st)
        rstd = k.sbuf(f"ln_rstd{tag}", [SQ, NB], F32, st)
        eps = k.sbuf(f"ln_eps{tag}", [SQ, 1], F32, st)
        xn = k.sbuf(f"ln_xn{tag}", [SQ, NB, D], F32, st)
        stat_s, var_s, std_s, rstd_s, norm_s, turn_s, high_s, low_s = (
            k.sem(st, f"ln{tag}_{n}") for n in ("stat", "var", "std", "rstd", "norm", "turned", "high", "low"))
        with nc.Block() as block:
            @block.vector
            def _(dve):
                nc.vector.memset(eps[:], EPS).then_inc(stat_s, 1)
                for b in range(NB):
                    nc.vector.bn_stats(stats[:, b, :], k.x[:, b, :]).then_inc(stat_s, 1)
                for b in range(NB):
                    dve.wait_ge(stat_s, b + 2)
                    nc.vector.bn_aggr(mv[:, b, :], stats[:, b, :]).then_inc(var_s, 1)
                dve.wait_ge(std_s, 1)
                nc.vector.reciprocal(rstd[:], std[:]).then_inc(rstd_s, 1)
                dve.wait_ge(rstd_s, 1)
                dve.wait_ge(var_s, NB)
                for b in range(NB):
                    nc.vector.tensor_scalar(xn[:, b, :], k.x[:, b, :], mv[:, b, 0:1], rstd[:, b:b + 1],
                                            ALU.subtract, ALU.mult).then_inc(norm_s, 1)
                with dve.Fori(0, NB // GRP // 4) as j:
                    for g in range(4):
                        dve.wait_ge(high_s, 4 * j + g + 1)
                        low = k.xnL[:, :, ds(j * 4 * GRP * SQ + g * GRP * SQ, GRP * SQ)]
                        high = k.xnH[:, :, ds(j * 4 * GRP * SQ + g * GRP * SQ, GRP * SQ)]
                        nc.vector.tensor_tensor(low, P[:, g, 0:KT * GRP * SQ].rearrange("p (t n) -> p t n", t=KT),
                                                high.bitcast(F32), ALU.subtract).then_inc(low_s, 1)

            @block.scalar
            def _(act):
                act.wait_ge(var_s, NB)
                act.wait_ge(stat_s, 1)
                nc.scalar.activation(std[:], mv[:, :, 1], ACT.Sqrt, bias=eps[:, 0:1]).then_inc(std_s, 1)
                with act.Fori(0, NB // GRP // 4) as j:
                    for g in range(4):
                        act.wait_ge(turn_s, 4 * j + g + 1)
                        nc.scalar.copy(k.xnH[:, :, ds(j * 4 * GRP * SQ + g * GRP * SQ, GRP * SQ)],
                                       P[:, g, 0:KT * GRP * SQ].rearrange("p (t n) -> p t n", t=KT)).then_inc(high_s, 1)

            @block.tensor
            def _(pe):
                for g in range(NB // GRP):
                    pe.wait_ge(norm_s, GRP * (g + 1))
                    if g >= 4:
                        pe.wait_ge(low_s, g - 3)
                    for kt in range(KT):
                        for i in range(GRP):
                            c = (kt * GRP + i) * SQ
                            last = nc.tensor.transpose(P[:, g % 4, c:c + SQ],
                                                       xn[:, GRP * g + i, kt * 128:(kt + 1) * 128],
                                                       k.ident[0:SQ, 0:SQ])
                    last.then_inc(turn_s, 1)



def queries_0(k, wa):
    nc, P = k.nc, k.psum
    waH, waL = wa
    NPR, BUF = NH // 2, 4
    with ExitStack() as st:
        qs = [k.sbuf(f"q0_out{i}", [128, 4, 2, 4, SQ], F32R, st) for i in range(2)]
        prod_s, high_s, low_s = (k.sem(st, f"q0_{n}") for n in ("prod", "high", "low"))
        stored = [k.sem(st, f"q0_stored{i}") for i in range(2)]
        with nc.Block() as block:
            @block.tensor
            def _(pe):
                pe.sem_inc(low_s, BUF)
                with pe.Fori(0, NCH) as c:
                    for p in range(NPR):
                        pe.wait_ge(low_s, NPR * c + p + 1)
                        for kt in range(KT):
                            wH, wL = (w[:, kt, p * 128:(p + 1) * 128] for w in (waH, waL))
                            xH, xL = (x[:, kt, ds(c * CH, CH)] for x in (k.xnH, k.xnL))
                            out = P[:, p % BUF, 0:CH]
                            nc.tensor.matmul(out, wH, xH, start=(kt == 0), stop=False)
                            nc.tensor.matmul(out, wH, xL, start=False, stop=False)
                            last = nc.tensor.matmul(out, wL, xH, start=False, stop=(kt == KT - 1))
                        last.then_inc(prod_s, 1)

            @block.scalar
            def _(act):
                for i in range(2):
                    act.sem_inc(stored[i], 32)
                with act.Fori(0, NCH) as c:
                    for p in range(NPR):
                        act.wait_ge(prod_s, NPR * c + p + 1)
                        if p % 4 == 0:
                            act.wait_ge(stored[p // 4], 32 * c + 32)
                        nc.scalar.copy(qs[p // 4][:, :, 0, p % 4, :], by_sequence(P[:, p % BUF, 0:CH])).then_inc(high_s, 1)

            @block.vector
            def _(dve):
                with dve.Fori(0, NCH) as c:
                    for p in range(NPR):
                        dve.wait_ge(high_s, NPR * c + p + 1)
                        nc.vector.tensor_tensor(qs[p // 4][:, :, 1, p % 4, :], by_sequence(P[:, p % BUF, 0:CH]),
                                                qs[p // 4][:, :, 0, p % 4, :].bitcast(F32), ALU.subtract).then_inc(low_s, 1)

            @block.sync
            def _(sp):
                with sp.Fori(0, NCH) as c:
                    for i in range(2):
                        sp.wait_ge(low_s, NPR * c + 4 * i + 4 + BUF)
                        store_queries(k, sp, qs[i], c, i, stored[i])
                for i in range(2):
                    sp.wait_ge(stored[i], 32 + 32 * NCH)


def by_sequence(tile):
    return tile.rearrange("p (b q) -> p b q", b=4)


def store_queries(k, sp, qs, c, quad, stored):
    for hh in range(2):
        h0 = 8 * hh + 4 * quad
        sp.dma_start(k.dram["q_lat"][ds(4 * c, 4), :, :, h0:h0 + 4, :].rearrange("b l d h q -> d (b l) (h q)"),
                     qs[64 * hh:64 * hh + 64].rearrange("p b l h q -> p (b l) (h q)").bitcast(F32)).then_inc(stored, 16)


class Count:

    AHEAD = 2

    def __init__(self, k, stack, name, per, unit=1):
        self.sem, self.per, self.unit = k.sem(stack, name), per, unit

    def start(self, eng):
        eng.sem_inc(self.sem, self.AHEAD * self.per * self.unit)

    def upto(self, b, i=0):
        return (b + self.AHEAD) * (self.per * self.unit) + (i + 1) * self.unit


def wait(eng, count, b, i=0):
    eng.wait_ge(count.sem, count.upto(b, i))


def pipelined(eng, body, heads=1, peel_last=False):
    body(0, None, 0, 0, None)
    if heads == 2:
        body(1, 0, 1, 0, 0)
        with eng.Fori(0, NB // 2 - 1 - peel_last) as j:
            body(2 * j + 2, 2 * j + 1, 0, j + 1, j)
            body(2 * j + 3, 2 * j + 2, 1, j + 1, j + 1)
        if peel_last:
            body(NB - 2, NB - 3, 0, NB // 2 - 1, NB // 2 - 2)
            body(NB - 1, NB - 2, 1, NB // 2 - 1, NB // 2 - 1)
        body(None, NB - 1, 0, None, NB // 2 - 1)
        return
    with eng.Fori(0, (NB - 2) // 2) as j:
        body(2 * j + 1, 2 * j, 1, j, j)
        body(2 * j + 2, 2 * j + 1, 0, j + 1, j)
    body(NB - 1, NB - 2, 1, NB // 2 - 1, NB // 2 - 1)
    body(None, NB - 1, 0, None, NB // 2 - 1)



def attention_0(k, v0, maskq, identb):
    nc, P = k.nc, k.psum
    with ExitStack() as st:
        ctx = [k.sbuf(f"a0_ctx{i}", [SQ, DC], F32, st) for i in range(2)]
        ctx2 = [k.sbuf(f"a0_ctx2{i}", [SQ, 2, DC], F32, st) for i in range(2)]
        qA = [k.sbuf(f"a0_qA{i}", [128, HQ], F32R, st) for i in range(2)]
        qH = [k.sbuf(f"a0_qH{i}", [DC, HQ], F32R, st) for i in range(2)]
        kHH = k.sbuf("a0_kHH", [128, SQ], F32R, st)
        kL = k.sbuf("a0_kL", [DC, SQ], F32R, st)
        mx = k.sbuf("a0_max", [SQ, NH], F32, st)
        den = k.sbuf("a0_den", [SQ, NH], F32, st)
        rden = k.sbuf("a0_rden", [SQ, NH], F32, st)
        e = [k.sbuf(f"a0_e{i}", [SQ, NH, SQ], F32, st) for i in range(2)]
        pt = [k.sbuf(f"a0_pt{i}", [SQ, CH], F32, st) for i in range(4)]
        cc = k.sbuf("a0_cc", [128, 2, CH], F32, st)

        def count(name, per, unit=1):
            return Count(k, st, f"a0_{name}", per, unit)

        ctx_in = [count(f"ctx_in{i}", 1, 16) for i in range(2)]
        ctx2_in = [count(f"ctx2_in{i}", 1, 32) for i in range(2)]
        q_in = [count(f"q_in{i}", 1, 32) for i in range(2)]
        kturn, khigh, klow = count("kturn", 1), count("khigh", 1), count("klow", 1)
        score, maxed, shifted = count("score", 2), count("maxed", 2), count("shifted", 2)
        exped, summed, inverse, prob = count("exped", 2), count("summed", 2), count("inverse", 1), count("prob", 2)
        turned, pt_ready, pv, cc_ready = count("turned", 4), count("pt_ready", 4), count("pv", 2), count("cc_ready", 2)
        proj, added = count("proj", 1), count("added", 1)
        HB = NH // 2

        def follows(a):
            return not (isinstance(a, int) and a == NB - 1)

        def score_banks(half):
            return P[0:SQ, 2 * half:2 * half + 2, 0:CH].rearrange("q b (h s) -> q b h s", h=4)

        def by_bank(tile, half):
            return tile[:, HB * half:HB * half + HB].rearrange("q (b h) -> q b h", b=2)

        with nc.Block() as block:
            @block.sync
            def _(sp):
                for c in ctx_in + ctx2_in + q_in:
                    c.start(sp)
                with sp.Fori(0, NB // 2) as j:
                    for par in range(2):
                        a = 2 * j + par
                        wait(sp, kturn, a - 2)
                        for i in range(2):
                            sp.dma_start(ctx2[par][:, i, :], k.dram["ctx"][ds(a, 1), 0:SQ, :].rearrange("o s d -> (o s) d")
                                         ).then_inc(ctx2_in[par].sem, 16)
                        wait(sp, score, a - 2, 1)
                        src = k.dram["q_lat"][ds(a, 1)]
                        sp.dma_start(qA[par][:].bitcast(F32), src.rearrange("o l d h q -> (o l d) (h q)")
                                     ).then_inc(q_in[par].sem, 16)
                        sp.dma_start(qH[par][:].bitcast(F32), src[:, 0].rearrange("o d h q -> (o d) (h q)")
                                     ).then_inc(q_in[par].sem, 16)
                        wait(sp, pv, a - 2, 1)
                        sp.dma_start(ctx[par][:], k.dram["ctx"][ds(a, 1), 0:SQ, :].rearrange("o s d -> (o s) d")
                                     ).then_inc(ctx_in[par].sem, 16)

            @block.tensor
            def _(pe):
                for c in (kturn, score, turned, pv, proj):
                    c.start(pe)

                def turn_keys(a, par, half_a):
                    wait(pe, ctx2_in[par], half_a)
                    if not (isinstance(a, int) and a < 3):
                        wait(pe, cc_ready, a - 3, 1)
                    nc.tensor.transpose(P[:, 7, 0:SQ], ctx2[par][:].rearrange("s i d -> s (i d)"),
                                        k.ident[0:SQ, 0:SQ]).then_inc(kturn.sem, 1)

                def scores(a, par, half_a, half):
                    if half == 0:
                        wait(pe, q_in[par], half_a)
                        wait(pe, khigh, a)
                        wait(pe, klow, a)
                    wait(pe, shifted, a - 1, half)
                    for bank in (2 * half, 2 * half + 1):
                        nc.tensor.matmul(P[0:SQ, bank, 0:CH], identb[0:SQ, 0:SQ],
                                         maskq[:].rearrange("q (o s) -> q o s", o=1).to_broadcast([SQ, 4, SQ]),
                                         start=True, stop=True, skip_group_check=True)
                        for i in range(4):
                            h = 4 * bank + i
                            out = P[0:SQ, bank, i * SQ:(i + 1) * SQ]
                            nc.tensor.matmul(out, qA[par][:, h * SQ:(h + 1) * SQ], kHH[:], start=False, stop=False,
                                             skip_group_check=True)
                            last = nc.tensor.matmul(out, qH[par][:, h * SQ:(h + 1) * SQ], kL[:], start=False,
                                                    stop=True, skip_group_check=True)
                    last.then_inc(score.sem, 1)

                def turn_probs(b, par, i):
                    wait(pe, prob, b, i // 2)
                    if i < 2:
                        wait(pe, pt_ready, b - 1, i + 2)
                    else:
                        wait(pe, pt_ready, b, i - 2)
                    for h in range(4):
                        last = nc.tensor.transpose(P[0:SQ, 4 + i % 2, h * SQ:(h + 1) * SQ], e[par][:, 4 * i + h, :],
                                                   k.ident[0:SQ, 0:SQ])
                    last.then_inc(turned.sem, 1)

                def times_ctx(a, b, par, half_b, i):
                    wait(pe, pt_ready, b, 2 * i + 1)
                    wait(pe, ctx_in[par], half_b)
                    if i == 0:
                        wait(pe, added, b - 1)
                    elif a is None:
                        wait(pe, klow, b)
                    else:
                        wait(pe, klow, a + 1 if follows(a) else a)
                    for up in range(2):
                        last = nc.tensor.matmul(P[64 * up:64 * up + 64, 6 + i, 0:CH], ctx[par][:], pt[2 * i + up][:],
                                                start=True, stop=True)
                    last.then_inc(pv.sem, 1)

                def project(b):
                    wait(pe, cc_ready, b, 1)
                    for p in range(8):
                        last = nc.tensor.matmul(P[0:SQ, 6, 0:D], cc[:, p // 4, (p % 4) * SQ:(p % 4 + 1) * SQ],
                                                v0[:, p, :], start=(p == 0), stop=(p == 7))
                    last.then_inc(proj.sem, 1)

                def body(a, b, par, ha, hb):
                    if a is not None:
                        scores(a, par, ha, 0)
                    if b is not None:
                        turn_probs(b, 1 - par, 0)
                        turn_probs(b, 1 - par, 1)
                    if a is not None:
                        scores(a, par, ha, 1)
                        if follows(a):
                            turn_keys(a + 1, 1 - par, ha + par)
                    if b is not None:
                        turn_probs(b, 1 - par, 2)
                        turn_probs(b, 1 - par, 3)
                        if not (isinstance(b, int) and b == 0):
                            project(b - 1)
                        times_ctx(a, b, 1 - par, hb, 0)
                        times_ctx(a, b, 1 - par, hb, 1)
                        if a is None:
                            project(b)

                turn_keys(0, 0, 0)
                pipelined(pe, body, heads=2, peel_last=True)

            @block.scalar
            def _(act):
                for c in (khigh, exped, pt_ready):
                    c.start(act)

                def high_keys(a):
                    wait(act, kturn, a)
                    wait(act, score, a - 1, 1)
                    nc.scalar.copy(kHH[:], P[:, 7, 0:SQ]).then_inc(khigh.sem, 1)

                def exp_half(a, par, half):
                    wait(act, shifted, a, half)
                    tile = e[par][:, HB * half:HB * half + HB, :]
                    nc.scalar.activation(tile, tile, ACT.Exp).then_inc(exped.sem, 1)

                def body(a, b, par, ha, hb):
                    for half in range(2):
                        if b is not None:
                            for i in (2 * half, 2 * half + 1):
                                wait(act, turned, b, i)
                                wait(act, pv, b - 1, i // 2)
                                nc.scalar.copy(pt[i][:], P[0:SQ, 4 + i % 2, 0:CH]).then_inc(pt_ready.sem, 1)
                        if a is not None:
                            if half == 0 and follows(a):
                                high_keys(a + 1)
                            exp_half(a, par, half)

                high_keys(0)
                pipelined(act, body, heads=2, peel_last=True)

            @block.vector
            def _(dve):
                for c in (klow, maxed, shifted, summed, inverse, cc_ready, added):
                    c.start(dve)

                def shift(a, par, half):
                    wait(dve, score, a, half)
                    wait(dve, shifted, a - 1, half)
                    nc.vector.tensor_reduce(by_bank(mx, half), score_banks(half), AX.X, ALU.max).then_inc(maxed.sem, 1)
                    wait(dve, maxed, a, half)
                    wait(dve, turned, a - 2, 3)
                    nc.vector.tensor_tensor(e[par][:, HB * half:HB * half + HB, :].rearrange("q (b h) s -> q b h s", b=2),
                                            score_banks(half),
                                            by_bank(mx, half).rearrange("q b (h o) -> q b h o", o=1).to_broadcast([SQ, 2, 4, SQ]),
                                            ALU.subtract).then_inc(shifted.sem, 1)

                def keep(b, i):
                    wait(dve, pv, b, i)
                    wait(dve, proj, b - 1)
                    nc.vector.tensor_copy(cc[:, i, :], P[:, 6 + i, 0:CH]).then_inc(cc_ready.sem, 1)

                def low_keys(a):
                    wait(dve, khigh, a)
                    wait(dve, score, a - 1, 1)
                    nc.vector.tensor_tensor(kL[:], P[0:DC, 7, 0:SQ], kHH[0:DC, :].bitcast(F32),
                                            ALU.subtract).then_inc(klow.sem, 1)

                def add(b):
                    wait(dve, proj, b)
                    xb = k.x[:, ds(b, 1), :].rearrange("q o d -> q (o d)")
                    nc.vector.scalar_tensor_tensor(out=xb, in0=P[0:SQ, 6, 0:D], scalar=k.gates[0:SQ, 0:1], in1=xb,
                                                   op0=ALU.mult, op1=ALU.add).then_inc(added.sem, 1)

                def body(a, b, par, ha, hb):
                    if a is not None:
                        shift(a, par, 0)
                        shift(a, par, 1)
                        if follows(a):
                            low_keys(a + 1)
                        for half in range(2):
                            wait(dve, exped, a, half)
                            wait(dve, inverse, a - 1)
                            nc.vector.tensor_reduce(den[:, HB * half:HB * half + HB], e[par][:, HB * half:HB * half + HB, :],
                                                    AX.X, ALU.add).then_inc(summed.sem, 1)
                        wait(dve, summed, a, 1)
                        wait(dve, prob, a - 1, 1)
                        nc.vector.reciprocal(rden[:], den[:]).then_inc(inverse.sem, 1)
                    if b is not None:
                        if not (isinstance(b, int) and b == 0):
                            add(b - 1)
                        keep(b, 0)
                        keep(b, 1)
                        if a is None:
                            add(b)

                low_keys(0)
                pipelined(dve, body, heads=2, peel_last=True)

            @block.gpsimd
            def _(pool):
                prob.start(pool)

                def body(a, b, par, ha, hb):
                    if a is None:
                        return
                    wait(pool, inverse, a)
                    for half in range(2):
                        tile = e[par][:, HB * half:HB * half + HB, :]
                        nc.gpsimd.tensor_tensor(tile, tile, rden[:, HB * half:HB * half + HB].rearrange("q (h o) -> q h o", o=1)
                                                .to_broadcast([SQ, HB, SQ]), ALU.mult).then_inc(prob.sem, 1)

                pipelined(pool, body)



def route(k, tag, n_exp, n_group, top_group, top_k, router, bias, fill, tiny):
    nc, P = k.nc, k.psum
    E2, SCALE, per = n_exp + 2, 2.5, n_exp // n_group
    with ExitStack() as st:
        def sb(name, shape, dt=F32):
            return k.sbuf(f"r{tag}_{name}", shape, dt, st)

        raw, rH, rL = sb("raw", [128, KT, n_exp]), sb("rH", [128, KT, n_exp], F32R), sb("rL", [128, KT, n_exp], F32R)
        bias_sb = sb("bias", [SQ, n_exp])
        ex, score = sb("ex", [SQ, NB, n_exp]), sb("score", [SQ, NB, n_exp])
        choice = sb("choice", [SQ, NB, n_exp])
        pair = [sb(f"pair{i}", [SQ, NB, n_group, 2]) for i in range(2)]
        two = [sb(f"two{i}", [SQ, NB, n_group]) for i in range(3)]
        gsum, gkeep = sb("gsum", [SQ, NB, n_group]), sb("gkeep", [SQ, NB, n_group])
        glow, gcmp, gcmp2 = sb("glow", [SQ, n_group, n_group]), sb("gcmp", [SQ, NB, n_group, n_group]), sb("gcmp2", [SQ, NB, n_group, n_group])
        masked, top8, rest = sb("masked", [SQ, NB, n_exp]), sb("top8", [SQ, NB, 8]), sb("rest", [SQ, NB, n_exp])
        wsum, wall = sb("wsum", [SQ, NB]), sb("wall", [SQ, NB, E2])
        wT = sb("wT", [E2, T])
        loaded, logit, sig, turned, moved, stored = (k.sem(st, f"r{tag}_{n}") for n in
                                                     ("loaded", "logit", "sig", "turned", "moved", "stored"))
        split, step, weights = (k.sem(st, f"r{tag}_{n}") for n in ("split", "step", "weights"))
        n_step = [0]
        with nc.Block() as block:
            @block.sync
            def _(sp):
                sp.dma_start(raw[:], router).then_inc(loaded, 16)
                sp.dma_start(bias_sb[:], bias.partition_broadcast(SQ)).then_inc(loaded, 16)
                sp.dma_start(glow[:], k.dram[f"earlier{n_group}"].partition_broadcast(SQ)).then_inc(loaded, 16)
                sp.wait_ge(moved, NB // 4)
                sp.dma_start(k.dram["route"][0:E2, :], wT[:]).then_inc(stored, 16)
                sp.wait_ge(stored, 16)

            @block.tensor
            def _(pe):
                pe.wait_ge(split, 2)
                for b in range(NB):
                    out = P[0:SQ, 0, b * n_exp:(b + 1) * n_exp]
                    n = 0
                    for kt in range(KT):
                        for x in (k.xnH, k.xnL):
                            for r in (rH, rL):
                                last = nc.tensor.matmul(out, x[:, kt, b * SQ:(b + 1) * SQ], r[:, kt, :],
                                                        start=(n == 0), stop=(n == 7))
                                n += 1
                last.then_inc(logit, 1)
                pe.wait_ge(weights, 1)
                for b in range(NB):
                    last = nc.tensor.transpose(P[0:E2, 1 + b // 4, (b % 4) * SQ:(b % 4 + 1) * SQ], wall[:, b, :],
                                               k.ident[0:SQ, 0:SQ])
                    if b % 4 == 3:
                        last.then_inc(turned, 1)

            @block.scalar
            def _(act):
                act.wait_ge(logit, 1)
                nc.scalar.activation(ex[:].rearrange("q b e -> q (b e)"), P[0:SQ, 0, 0:NB * n_exp], ACT.Exp, scale=-1.0
                                     ).then_inc(sig, 1)
                for i in range(NB // 4):
                    act.wait_ge(turned, i + 1)
                    nc.scalar.copy(wT[:, i * CH:(i + 1) * CH], P[0:E2, 1 + i, 0:CH]).then_inc(moved, 1)

            @block.vector
            def _(dve):
                def then(ins):
                    n_step[0] += 1
                    ins.then_inc(step, 1)
                    dve.wait_ge(step, n_step[0])

                def rank(values, n, earlier, cmp, cmp2, out):
                    shape = [SQ, NB, n, n]
                    this = values[:].rearrange("q b (g o) -> q b g o", o=1).to_broadcast(shape)
                    other = values[:].rearrange("q b (o g) -> q b o g", o=1).to_broadcast(shape)
                    early = earlier[:].rearrange("q (o g) h -> q o g h", o=1).to_broadcast(shape)
                    then(nc.vector.tensor_tensor(cmp[:], other, this, ALU.is_equal))
                    then(nc.vector.tensor_tensor(cmp[:], cmp[:], early, ALU.mult))
                    then(nc.vector.tensor_tensor(cmp2[:], other, this, ALU.is_gt))
                    then(nc.vector.tensor_tensor(cmp[:], cmp[:], cmp2[:], ALU.add))
                    then(nc.vector.tensor_reduce(out[:], cmp[:], AX.X, ALU.add))

                dve.wait_ge(loaded, 48)
                nc.vector.tensor_copy(rH[:], raw[:]).then_inc(split, 1)
                dve.wait_ge(split, 1)
                nc.vector.tensor_tensor(rL[:], raw[:], rH[:].bitcast(F32), ALU.subtract).then_inc(split, 1)
                dve.wait_ge(sig, 1)
                then(nc.vector.tensor_scalar(ex[:], ex[:], 1.0, None, ALU.add))
                then(nc.vector.reciprocal(score[:], ex[:]))
                then(nc.vector.tensor_tensor(choice[:], score[:],
                                             bias_sb[:].rearrange("q (o e) -> q o e", o=1).to_broadcast([SQ, NB, n_exp]), ALU.add))
                quad = choice[:].rearrange("q b (g h e) -> q b g h e", g=n_group, h=2)
                for h in range(2):
                    for op, which in ((ALU.max, 0), (ALU.min, 1)):
                        then(nc.vector.tensor_tensor(pair[which][:, :, :, h], quad[:, :, :, h, 0], quad[:, :, :, h, 1], op))
                then(nc.vector.tensor_tensor(two[0][:], pair[0][:, :, :, 0], pair[0][:, :, :, 1], ALU.max))
                then(nc.vector.tensor_tensor(two[1][:], pair[0][:, :, :, 0], pair[0][:, :, :, 1], ALU.min))
                then(nc.vector.tensor_tensor(two[2][:], pair[1][:, :, :, 0], pair[1][:, :, :, 1], ALU.max))
                then(nc.vector.tensor_tensor(two[1][:], two[1][:], two[2][:], ALU.max))
                then(nc.vector.tensor_tensor(gsum[:], two[0][:], two[1][:], ALU.add))
                rank(gsum, n_group, glow, gcmp, gcmp2, gkeep)
                then(nc.vector.tensor_scalar(gkeep[:], gkeep[:], float(top_group), None, ALU.is_lt))
                keep4 = gkeep[:].rearrange("q b (g o) -> q b g o", o=1).to_broadcast([SQ, NB, n_group, per])
                then(nc.vector.tensor_tensor(masked[:].rearrange("q b (g e) -> q b g e", g=n_group),
                                             choice[:].rearrange("q b (g e) -> q b g e", g=n_group), keep4, ALU.mult))
                if fill:
                    then(nc.vector.tensor_scalar(gkeep[:], gkeep[:], -1.0, -LOWEST, ALU.add, ALU.mult))
                    then(nc.vector.tensor_tensor(masked[:].rearrange("q b (g e) -> q b g e", g=n_group),
                                                 masked[:].rearrange("q b (g e) -> q b g e", g=n_group), keep4, ALU.add))
                then(nc.vector.tensor_scalar(masked[:], masked[:], 0.0, None, ALU.add))
                for b in range(NB):
                    nc.vector.max(top8[:, b, :], masked[:, b, :]).then_inc(step, 1)
                n_step[0] += NB
                dve.wait_ge(step, n_step[0])
                if top_k < 8:
                    then(nc.vector.memset(top8[:, :, top_k:8], HIGHEST))
                for b in range(NB):
                    nc.vector.match_replace(rest[:, b, :], top8[:, b, :], masked[:, b, :], CHOSEN).then_inc(step, 1)
                n_step[0] += NB
                dve.wait_ge(step, n_step[0])
                then(nc.vector.tensor_scalar(rest[:], rest[:], CHOSEN, None, ALU.is_equal))
                then(nc.vector.tensor_tensor(rest[:], rest[:], score[:], ALU.mult))
                then(nc.vector.tensor_reduce(wsum[:], rest[:], AX.X, ALU.add))
                if tiny:
                    then(nc.vector.tensor_scalar(wsum[:], wsum[:], tiny, None, ALU.add))
                then(nc.vector.reciprocal(wsum[:], wsum[:]))
                then(nc.vector.tensor_scalar(wsum[:], wsum[:], SCALE, None, ALU.mult))
                then(nc.vector.memset(wall[:, :, n_exp:E2], 1.0))
                nc.vector.tensor_tensor(wall[:, :, 0:n_exp], rest[:],
                                        wsum[:].rearrange("q (b o) -> q b o", o=1).to_broadcast([SQ, NB, n_exp]),
                                        ALU.mult).then_inc(weights, 1)



class Tally:

    AHEAD = 4

    def __init__(self, k, stack, name, unit=1):
        self.sem, self.unit = k.sem(stack, name), unit

    def start(self, eng):
        eng.sem_inc(self.sem, self.AHEAD * self.unit)

    def upto(self, n):
        return (n + self.AHEAD + 1) * self.unit


def until(eng, tally, n):
    eng.wait_ge(tally.sem, tally.upto(n))


def experts(k, tag, n_exp, weights, gate):
    nc, P = k.nc, k.psum
    E2, HT = n_exp + 2, T // 2
    GU, NW = 4 * 128, 6 * 128
    with ExitStack() as st:
        def sb(name, shape, dt=F32):
            return k.sbuf(f"m{tag}_{name}", shape, dt, st)

        def tally(name, unit=1):
            return Tally(k, st, f"m{tag}_{name}", unit)

        wraw = [sb(f"wraw{i}", [128, NW]) for i in range(2)]
        wH = [sb(f"wH{i}", [128, NW], F32R) for i in range(2)]
        wL = [sb(f"wL{i}", [128, NW], F32R) for i in range(2)]
        row = [sb(f"row{i}", [1, HT]) for i in range(2)]
        wide = [sb(f"wide{i}", [128, HT]) for i in range(2)]
        sg = [sb(f"sg{i}", [128, CH]) for i in range(2)]
        act_ = [sb(f"act{i}", [128, CH]) for i in range(2)]
        aH = [sb(f"aH{i}", [128, CH], F32R) for i in range(4)]
        aL = [sb(f"aL{i}", [128, CH], F32R) for i in range(4)]
        y = sb("y", [128, KT, 2, CH])
        w_in, row_in = [tally(f"w_in{i}", 16) for i in range(2)], [tally(f"row_in{i}", 16) for i in range(2)]
        gu_high, gu_low, d_high, d_low, spread = (tally(x) for x in ("gu_high", "gu_low", "d_high", "d_low", "spread"))
        gated, upped, silu, weighed, acted, a_high, a_low, downed = (
            tally(x) for x in ("gated", "upped", "silu", "weighed", "acted", "a_high", "a_low", "downed"))
        row_ok = tally("row_ok")
        y_kept, y_turned, added = tally("y_kept"), tally("y_turned"), tally("added")

        def halves(eng, body, tail):
            for half in range(2):
                n0 = half * E2
                body(n0, 0, True)
                body(n0 + 1, 1, None)
                with eng.Fori(1, E2 // 2) as j:
                    body(2 * j + n0, 0, False)
                    body(2 * j + n0 + 1, 1, False)
                tail(n0 + E2 - 1, half)

        with nc.Block() as block:
            @block.sync
            def _(sp):
                for i in range(2):
                    w_in[i].start(sp)
                    row_in[i].start(sp)
                for half in range(2):
                    with sp.Fori(0, E2 // 2) as j:
                        for par in range(2):
                            n = 2 * j + (half * E2 + par)
                            until(sp, gu_high, n - 2)
                            until(sp, gu_low, n - 2)
                            until(sp, d_high, n - 2)
                            until(sp, d_low, n - 2)
                            sp.dma_start(wraw[par][:], weights[ds(2 * j + par, 1)].rearrange("o p n -> (o p) n")
                                         ).then_inc(w_in[par].sem, 16)
                            until(sp, spread, n - 2)
                            sp.dma_start(row[par][:], k.dram["route"][ds(2 * j + par, 1), half * HT:(half + 1) * HT]
                                         ).then_inc(row_in[par].sem, 16)

            @block.tensor
            def _(pe):
                for t in (gated, upped, downed, y_turned):
                    t.start(pe)

                def project(par, c, half_c, bank, tally_, lo, u):
                    for kt in range(KT):
                        w = slice(lo + kt * 128, lo + (kt + 1) * 128)
                        xH, xL = (x[:, kt, half_c] for x in (k.xnH, k.xnL))
                        out = P[:, bank, 0:CH]
                        nc.tensor.matmul(out, wH[par][:, w], xH, start=(kt == 0), stop=False)
                        nc.tensor.matmul(out, wH[par][:, w], xL, start=False, stop=False)
                        last = nc.tensor.matmul(out, wL[par][:, w], xH, start=False, stop=(kt == KT - 1))
                    last.then_inc(tally_.sem, 1)

                def down(n, par, c, start, stop):
                    u = 2 * n + c
                    until(pe, d_high, n)
                    until(pe, d_low, n)
                    until(pe, a_low, u)
                    i = 2 * par + c
                    for m in range(KT):
                        w = slice(GU + m * 128, GU + (m + 1) * 128)
                        out = P[:, 2 * m + c, 0:CH]
                        nc.tensor.matmul(out, wH[par][:, w], aH[i][:], start=start, stop=False, skip_group_check=True)
                        nc.tensor.matmul(out, wH[par][:, w], aL[i][:], start=False, stop=False, skip_group_check=True)
                        last = nc.tensor.matmul(out, wL[par][:, w], aH[i][:], start=False, stop=stop, skip_group_check=True)
                    last.then_inc(downed.sem, 1)

                def body(n, par, first):
                    half = current[0]
                    if first is True and half:
                        until(pe, added, 3)
                    until(pe, gu_high, n)
                    until(pe, gu_low, n)
                    for c in range(2):
                        u = 2 * n + c
                        cols = slice(half * HT + c * CH, half * HT + (c + 1) * CH)
                        until(pe, silu, u - 2)
                        project(par, c, cols, 4 + c, gated, 0, u)
                        until(pe, acted, u - 2)
                        project(par, c, cols, 6 + c, upped, 2 * 128, u)
                        if first is not True:
                            if first is None and c == 0 and half:
                                until(pe, y_kept, half - 1)
                            down(n - 1, 1 - par, c, first is None, False)

                def tail(n, half):
                    for c in range(2):
                        down(n, 1, c, False, True)
                    until(pe, y_kept, half)
                    until(pe, acted, 2 * n + 1)
                    for i in range(4):
                        for s in range(2):
                            tok = (2 * i + s) * SQ
                            for m in range(KT):
                                last = nc.tensor.transpose(P[0:SQ, 4 + i, s * D + m * 128:s * D + (m + 1) * 128],
                                                           y[:, m, tok // CH, tok % CH:tok % CH + SQ], k.ident[:])
                        last.then_inc(y_turned.sem, 1)
                    current[0] += 1

                current = [0]
                halves(pe, body, tail)

            @block.scalar
            def _(act):
                for t in (gu_high, d_high, silu, y_kept):
                    t.start(act)

                def silu_of(u, c):
                    until(act, gated, u)
                    until(act, acted, u - 2)
                    nc.scalar.activation(sg[c][:], P[:, 4 + c, 0:CH], ACT.Silu).then_inc(silu.sem, 1)

                def body(n, par, first):
                    act.wait_ge(w_in[par].sem, load_count(n, par, w_in[par]))
                    until(act, upped, 2 * n - 3)
                    nc.scalar.copy(wH[par][:, 0:GU], wraw[par][:, 0:GU]).then_inc(gu_high.sem, 1)
                    if first is not True:
                        silu_of(2 * n - 1, 1)
                    until(act, downed, 2 * n - 3)
                    nc.scalar.copy(wH[par][:, GU:NW], wraw[par][:, GU:NW]).then_inc(d_high.sem, 1)
                    silu_of(2 * n, 0)

                def tail(n, half):
                    silu_of(2 * n + 1, 1)
                    until(act, downed, 2 * n + 1)
                    if half:
                        until(act, y_turned, 3)
                    nc.scalar.copy(y[:].rearrange("p m c n -> p (m c) n"), P[:, 0:4, 0:CH]).then_inc(y_kept.sem, 1)

                def load_count(n, par, t):
                    return t.upto(0) + (n - par) * 8

                halves(act, body, tail)

            @block.gpsimd
            def _(pool):
                spread.start(pool)
                weighed.start(pool)

                def body(n, par, first):
                    pool.wait_ge(row_in[par].sem, row_in[par].upto(0) + (n - par) * 8)
                    until(pool, weighed, 2 * n - 3)
                    pool.sem_inc(row_ok.sem)
                    nc.gpsimd.partition_broadcast(wide[par][:], row[par][:]).then_inc(spread.sem, 1)
                    until(pool, spread, n)
                    for c in range(2):
                        until(pool, silu, 2 * n + c)
                        nc.gpsimd.tensor_tensor(sg[c][:], sg[c][:], wide[par][:, c * CH:(c + 1) * CH], ALU.mult
                                                ).then_inc(weighed.sem, 1)

                halves(pool, body, lambda n, half: None)

            @block.vector
            def _(dve):
                for t in (gu_low, d_low, acted, a_high, a_low, added):
                    t.start(dve)

                def act_of(n, par, c):
                    u, i = 2 * n + c, 2 * par + c
                    until(dve, weighed, u)
                    until(dve, upped, u)
                    until(dve, a_low, u - 2)
                    nc.vector.tensor_tensor(act_[c][:], sg[c][:], P[:, 6 + c, 0:CH], ALU.mult).then_inc(acted.sem, 1)
                    until(dve, acted, u)
                    until(dve, downed, u - 4)
                    nc.vector.tensor_copy(aH[i][:], act_[c][:]).then_inc(a_high.sem, 1)
                    until(dve, a_high, u)
                    nc.vector.tensor_tensor(aL[i][:], act_[c][:], aH[i][:].bitcast(F32), ALU.subtract).then_inc(a_low.sem, 1)

                def body(n, par, first):
                    until(dve, gu_high, n)
                    nc.vector.tensor_tensor(wL[par][:, 0:GU], wraw[par][:, 0:GU], wH[par][:, 0:GU].bitcast(F32),
                                            ALU.subtract).then_inc(gu_low.sem, 1)
                    if first is not True:
                        act_of(n - 1, 1 - par, 1)
                    until(dve, d_high, n)
                    nc.vector.tensor_tensor(wL[par][:, GU:NW], wraw[par][:, GU:NW], wH[par][:, GU:NW].bitcast(F32),
                                            ALU.subtract).then_inc(d_low.sem, 1)
                    act_of(n, par, 0)

                def tail(n, half):
                    act_of(n, 1, 1)
                    for i in range(4):
                        until(dve, y_turned, 4 * half + i)
                        for s in range(2):
                            b = 8 * half + 2 * i + s
                            last = nc.vector.scalar_tensor_tensor(out=k.x[:, b, :], in0=P[0:SQ, 4 + i, s * D:(s + 1) * D],
                                                                  scalar=k.gates[0:SQ, gate:gate + 1], in1=k.x[:, b, :],
                                                                  op0=ALU.mult, op1=ALU.add)
                        last.then_inc(added.sem, 1)

                halves(dve, body, tail)



def prepare_1(k, wa, mm, v1):
    nc, P = k.nc, k.psum
    waH, waL = wa
    with ExitStack() as st:
        wqk = k.sbuf("wqk1", [128, NH, D + DCQ], F32, st)
        wvo = k.sbuf("wvo1", [128, NH, DC + D], F32, st)
        wr = k.sbuf("wr1", [DC, NH, DCQ + DC], F32, st)
        in_qk, in_vo, in_r, qk, high, low, vo, vo_kept, rr, rr_kept = (
            k.sem(st, f"p1_{n}") for n in ("in_qk", "in_vo", "in_r", "qk", "high", "low", "vo", "vo_kept", "rr", "rr_kept"))
        with nc.Block() as block:
            @block.sync
            def _(sp):
                sp.dma_start(wqk[:], k.dram["wqk1"]).then_inc(in_qk, 16)
                sp.dma_start(wr[:], k.dram["wr1"]).then_inc(in_r, 16)
                sp.dma_start(wvo[:], k.dram["wvo1"]).then_inc(in_vo, 16)

            @block.tensor
            def _(pe):
                pe.wait_ge(in_qk, 16)
                for h in range(NH):
                    if h >= 4:
                        pe.wait_ge(low, h - 3)
                    for kt in range(KT):
                        last = nc.tensor.matmul(P[:, h % 4, kt * DCQ:(kt + 1) * DCQ], wqk[:, h, kt * 128:(kt + 1) * 128],
                                                wqk[:, h, D:], start=True, stop=True)
                    last.then_inc(qk, 1)
                pe.wait_ge(in_r, 16)
                for half in range(2):
                    if half:
                        pe.wait_ge(rr_kept, 1)
                    for h in range(NH):
                        last = nc.tensor.matmul(P[0:HALF, 6 + h // 8, (h % 8) * DC:(h % 8 + 1) * DC],
                                                wr[:, h, half * HALF:(half + 1) * HALF], wr[:, h, DCQ:], start=True, stop=True)
                    last.then_inc(rr, 1)
                pe.wait_ge(in_vo, 16)
                for i in range(NH // 2):
                    if i >= 4 and i % 2 == 0:
                        pe.wait_ge(vo_kept, i // 2 - 1)
                    for up in range(2):
                        h = 8 * (i // 4) + i % 4 + 4 * up
                        last = nc.tensor.matmul(P[64 * up:64 * up + 64, 4 + i // 2 % 2, (i % 2) * D:(i % 2 + 1) * D],
                                                wvo[:, h, 0:DC], wvo[:, h, DC:], start=True, stop=True)
                    if i % 2:
                        last.then_inc(vo, 1)

            def of_head(tile, h):
                return tile[:, :, h * DCQ:(h + 1) * DCQ]

            def bank(h):
                return P[:, h % 4, 0:KT * DCQ].rearrange("p (t n) -> p t n", t=KT)

            @block.scalar
            def _(act):
                for h in range(NH):
                    act.wait_ge(qk, h + 1)
                    nc.scalar.copy(of_head(waH, h), bank(h)).then_inc(high, 1)
                for i in range(NH // 4):
                    act.wait_ge(vo, i + 1)
                    nc.scalar.copy(v1[:, 2 * i:2 * i + 2, :].rearrange("p h n -> p (h n)"), P[:, 4 + i % 2, :]).then_inc(vo_kept, 1)

            @block.vector
            def _(dve):
                for h in range(NH):
                    dve.wait_ge(high, h + 1)
                    nc.vector.tensor_tensor(of_head(waL, h), bank(h), of_head(waH, h).bitcast(F32), ALU.subtract).then_inc(low, 1)
                for half in range(2):
                    dve.wait_ge(rr, half + 1)
                    nc.vector.tensor_copy(mm[:, half, :], P[0:HALF, 6:8, :].rearrange("p b n -> p (b n)")).then_inc(rr_kept, 1)



def queries_1(k, wa, mm):
    nc, P = k.nc, k.psum
    NPR = NH // 2
    with ExitStack() as st:
        rope = k.sbuf("q1_rope", [HALF, 2, 2, SQ], F32, st)
        prods = [[k.sbuf(f"q1_prod{hh}{half}", [HALF, 2, CH], F32, st) for half in range(2)] for hh in range(2)]
        roped = [k.sbuf(f"q1_roped{i}", [HALF, 2, 2, CH], F32, st) for i in range(2)]
        qs = [k.sbuf(f"q1_out{i}", [128, 4, 2, 4, SQ], F32R, st) for i in range(2)]
        rope_in = k.sem(st, "q1_rope_in")
        big, multiplied, added, lat, high, low = (Tally(k, st, f"q1_{n}") for n in ("big", "multiplied", "added", "lat", "high", "low"))
        stored = [Tally(k, st, f"q1_stored{i}", 32) for i in range(2)]

        def chunks(eng, body, tail):
            for p in range(NPR):
                body(0, p, p % 2, p == 0)
            with eng.Fori(1, NCH) as c:
                for p in range(NPR):
                    body(c, p, p % 2, False)
            tail()

        with nc.Block() as block:
            @block.tensor
            def _(pe):
                for t in (big, lat):
                    t.start(pe)

                def latent(g, par):
                    until(pe, added, 4 * g + 3)
                    until(pe, low, g - 2)
                    for half in range(2):
                        for hh in range(2):
                            last = nc.tensor.matmul(P[64 * hh:64 * hh + 64, 4 + par, 0:CH], mm_of(half, pair_done[0] + 8 * hh),
                                                    roped[par][:, hh, half, :], start=(half == 0), stop=(half == 1))
                    last.then_inc(lat.sem, 1)

                def mm_of(half, h):
                    return mm[:, half, h * DC:(h + 1) * DC]

                pair_done = [0]

                def body(c, p, par, first):
                    g = NPR * c + p
                    for hh in range(2):
                        h, i = p + 8 * hh, 2 * g + hh
                        until(pe, multiplied, 2 * (i - 2) + 1)
                        for half in range(2):
                            w = slice(h * DCQ + half * HALF, h * DCQ + (half + 1) * HALF)
                            out = P[0:HALF, 2 * hh + half, 0:CH]
                            for kt in range(KT):
                                xH, xL = (x[:, kt, ds(c * CH, CH)] for x in (k.xnH, k.xnL))
                                nc.tensor.matmul(out, wa[0][:, kt, w], xH, start=(kt == 0), stop=False)
                                nc.tensor.matmul(out, wa[0][:, kt, w], xL, start=False, stop=False)
                                last = nc.tensor.matmul(out, wa[1][:, kt, w], xH, start=False, stop=(kt == KT - 1))
                        last.then_inc(big.sem, 1)
                    if not first:
                        pair_done[0] = (p - 1) % NPR
                        latent(g - 1, 1 - par)

                def tail():
                    pair_done[0] = NPR - 1
                    latent(NPR * NCH - 1, 1)

                chunks(pe, body, tail)

            @block.vector
            def _(dve):
                for t in (multiplied, low):
                    t.start(dve)
                dve.wait_ge(rope_in, 16)

                def low_part(g, p):
                    par = p % 2
                    until(dve, high, g)
                    nc.vector.tensor_tensor(qs[p // 4][:, :, 1, p % 4, :], by_sequence(P[:, 4 + par, 0:CH]),
                                            qs[p // 4][:, :, 0, p % 4, :].bitcast(F32), ALU.subtract
                                            ).then_inc(low.sem, 1)

                def body(c, p, par, first):
                    g = NPR * c + p
                    for hh in range(2):
                        i = 2 * g + hh
                        until(dve, big, i)
                        until(dve, added, 2 * (i - 2) + 1)
                        for half in range(2):
                            nc.vector.tensor_tensor(
                                prods[hh][half][:].rearrange("p t (b q) -> p t b q", b=4),
                                P[0:HALF, 2 * hh + half, 0:CH].rearrange("p (t b q) -> p t b q", t=1, b=4).to_broadcast([HALF, 2, 4, SQ]),
                                rope[:, half].rearrange("p t (o q) -> p t o q", o=1).to_broadcast([HALF, 2, 4, SQ]),
                                ALU.mult).then_inc(multiplied.sem, 1)
                    if not first:
                        low_part(g - 1, (p - 1) % NPR)

                chunks(dve, body, lambda: low_part(NPR * NCH - 1, NPR - 1))

            @block.gpsimd
            def _(pool):
                added.start(pool)

                def body(c, p, par, first):
                    g = NPR * c + p
                    for hh in range(2):
                        i = 2 * g + hh
                        until(pool, multiplied, 2 * i + 1)
                        until(pool, lat, g - 2)
                        for half, op in ((0, ALU.subtract), (1, ALU.add)):
                            nc.gpsimd.tensor_tensor(roped[par][:, hh, half, :], prods[hh][0][:, half, :], prods[hh][1][:, half, :], op
                                                    ).then_inc(added.sem, 1)

                chunks(pool, body, lambda: None)

            @block.scalar
            def _(act):
                high.start(act)

                def body(c, p, par, first):
                    g = NPR * c + p
                    until(act, lat, g)
                    if p % 4 == 0:
                        until(act, stored[p // 4], c - 1)
                    nc.scalar.copy(qs[p // 4][:, :, 0, p % 4, :], by_sequence(P[:, 4 + par, 0:CH])).then_inc(high.sem, 1)

                chunks(act, body, lambda: None)

            @block.sync
            def _(sp):
                sp.dma_start(rope[:], k.dram["rope_q"]).then_inc(rope_in, 16)
                for t in stored:
                    t.start(sp)

                def body(c, p, par, first):
                    if p % 4 == 3:
                        until(sp, low, NPR * c + p)
                        store_queries(k, sp, qs[p // 4], c, p // 4, stored[p // 4].sem)

                def tail():
                    for t in stored:
                        until(sp, t, NCH - 1)

                chunks(sp, body, tail)



def attention_1(k, v1):
    nc, P = k.nc, k.psum
    NT = (HQ + 127) // 128
    PARTS, UB = 3, 4
    PK = 2 * ((SK + 2 * PARTS - 1) // (2 * PARTS))
    NU, NSLOT, NPAIR = PARTS * NT, NCH * NKT, NCH * NKT // 2
    PRE = 4
    CHAIN_STEPS = 16
    CHAIN, TURN_SHIFT = 38, 8
    unit_slots = {}
    for i in range(NU):
        unit_slots.setdefault(1 - PRE + i * (CHAIN + PRE - 1) // NU, []).append(i)

    def key_rows(t):
        return 128 if t < NKT - 1 else KREST

    with ExitStack() as st:
        def sb(name, shape, dt=F32):
            return k.sbuf(f"a1_{name}", shape, dt, st)

        def count(name, per, unit=1):
            return Count(k, st, f"a1_{name}", per, unit)

        rope = sb("rope", [128, 2, NKT, DC])
        ctx = [sb(f"ctx{i}", [128, NKT, DC]) for i in range(2)]
        byc, bys = sb("byc", [128, NKT, DC]), sb("bys", [128, NKT, DC])
        kv = [sb(f"kv{i}", [128, NKT, DC]) for i in range(2)]
        kv2 = sb("kv2", [128, NKT, 2 * DC])
        kHH = [sb(f"kHH{i}", [128, SK], F32R) for i in range(2)]
        kL = [sb(f"kL{i}", [DC + 2, SK], F32R) for i in range(2)]
        qA = [sb(f"qA{i}", [128, HQ], F32R) for i in range(2)]
        qH = [sb(f"qH{i}", [DC + 2, HQ], F32R) for i in range(2)]
        nmax, den = sb("nmax", [128, NT, PARTS]), sb("den", [128, NT, PARTS])
        nm, gap, egap = sb("nm", [128, NT]), sb("gap", [128, NT, PARTS]), sb("egap", [128, NT, PARTS])
        total, shift, shs = sb("total", [128, NT]), sb("shift", [128, NT]), sb("shs", [128, 2, NT], F32R)
        log0, part, delta, series = (sb(n, [128, NT]) for n in ("log0", "part", "delta", "series"))
        rows = sb("rows", [2 * NT, 128])
        pt = [sb(f"pt{i}", [128, 2, CH]) for i in range(3)]
        cc = sb("cc", [128, HQ // 2])

        cleared, ones_set = k.sem(st, "a1_cleared"), k.sem(st, "a1_ones_set")
        rope_in = k.sem(st, "a1_rope_in")
        ctx_in = [count(f"ctx_in{i}", 1, 32) for i in range(2)]
        q_in = [[count(f"q_in{i}{c}", 1, 32) for c in range(NCH)] for i in range(2)]
        shift_in = [count(f"shift_in{i}", 1, 16) for i in range(2)]
        shift_out = [count(f"shift_out{i}", 1, 16) for i in range(2)]
        times_cs, roped, roped2 = count("times_cs", 3), count("roped", 1), count("roped2", 2)
        kturn, khigh, klow = count("kturn", 2), count("khigh", 2), count("klow", 2)
        unit, umax, uexp = count("unit", NU), count("umax", NU), count("uexp", NU)
        chain_v, chain_a = count("chain_v", CHAIN_STEPS), count("chain_a", 2)
        sturn, srow = count("sturn", 1), count("srow", 1)
        scored, exped, pair = count("scored", NSLOT), count("exped", NSLOT), count("pair", NPAIR)
        cc_ready, proj, added = count("cc_ready", NCH // 2), count("proj", 1), count("added", 1)

        def key_banks(i):
            return P[:, 2 * i:2 * i + 2, :].rearrange("p b n -> p (b n)")

        SHIFT_BANK = UB - 1

        def unit_rows(i):
            return min(128, HQ - 128 * (i // PARTS))

        def unit_keys(i):
            return i % PARTS * PK, min(PK, SK - i % PARTS * PK)

        def unit_tile(i):
            return P[0:unit_rows(i), i % UB, 0:unit_keys(i)[1]]

        def of_unit(tile, i):
            return tile[0:unit_rows(i), i // PARTS, i % PARTS:i % PARTS + 1]

        def out_bank(par_b, i):
            return 6 + (3 * par_b + i) % 2

        def slot_work(s):
            return 2 * (s // (2 * NKT)) + s % 2, s % (2 * NKT) // 2

        with nc.Block() as block:
            @block.sync
            def _(sp):
                for c in ctx_in + q_in[0] + q_in[1] + shift_in + shift_out:
                    c.start(sp)
                sp.dma_start(rope[:], k.dram["rope_k"]).then_inc(rope_in, 16)
                sp.wait_ge(cleared, 1)

                def load_ctx(a, par):
                    wait(sp, times_cs, a - 2, 2)
                    src = k.dram["ctx"][ds(a, 1)].rearrange("o s d -> (o s) d")
                    sp.dma_start(ctx[par][:, 0:NKT - 1, :], src[0:128 * (NKT - 1)].rearrange("(t p) d -> p t d", p=128)
                                 ).then_inc(ctx_in[par].sem, 16)
                    sp.dma_start(ctx[par][0:KREST, NKT - 1, :], src[128 * (NKT - 1):SK]).then_inc(ctx_in[par].sem, 16)

                def load_q(a, par, c):
                    wait(sp, scored, a - 2, 2 * NKT * (c // 2 + 1) - 2 + c % 2)
                    src = k.dram["q_lat"][ds(a, 1), :, :, 4 * c:4 * c + 4, :]
                    sp.dma_start(qA[par][:, c * CH:(c + 1) * CH].bitcast(F32), src.rearrange("o l d h q -> (o l d) (h q)")
                                 ).then_inc(q_in[par][c].sem, 16)
                    sp.dma_start(qH[par][0:DC, c * CH:(c + 1) * CH].bitcast(F32), src[:, 0].rearrange("o d h q -> (o d) (h q)")
                                 ).then_inc(q_in[par][c].sem, 16)

                def spread_shift(a, par, ha):
                    wait(sp, srow, a)
                    sp.dma_start(k.dram["shift"][par].rearrange("l (t n) -> (l t) n", n=128), rows[:]
                                 ).then_inc(shift_out[par].sem, 16)
                    wait(sp, shift_out[par], ha)
                    sp.dma_start(qH[par][DC:DC + 2, :].bitcast(F32), k.dram["shift"][par, :, 0:HQ]).then_inc(shift_in[par].sem, 16)

                load_ctx(0, 0)
                for c in range(NCH):
                    load_q(0, 0, c)

                def body(a, b, par, ha, hb):
                    if a is None:
                        return
                    more = not (isinstance(a, int) and a == NB - 1)
                    if more:
                        load_ctx(a + 1, 1 - par)
                        for c in range(NCH // 2):
                            load_q(a + 1, 1 - par, c)
                    spread_shift(a, par, ha)
                    if more:
                        for c in range(NCH // 2, NCH):
                            load_q(a + 1, 1 - par, c)

                pipelined(sp, body)

            @block.gpsimd
            def _(pool):
                for c in (times_cs, roped, roped2):
                    c.start(pool)
                for i in range(2):
                    nc.gpsimd.memset(ctx[i][:], 0.0)
                nc.gpsimd.drain().then_inc(cleared, 1)
                pool.wait_ge(rope_in, 16)

                def products(a, par, ha):
                    wait(pool, ctx_in[par], ha)
                    wait(pool, roped, a - 1)
                    nc.gpsimd.tensor_tensor(byc[:], ctx[par][:], rope[:, 0], ALU.mult).then_inc(times_cs.sem, 1)
                    for i in range(2):
                        here, there = slice(32 * i, 32 * i + 32), slice(32 - 32 * i, 64 - 32 * i)
                        nc.gpsimd.tensor_tensor(bys[:, :, here], ctx[par][:, :, there], rope[:, 1, :, here], ALU.mult
                                                ).then_inc(times_cs.sem, 1)

                products(0, 0, 0)

                def body(a, b, par, ha, hb):
                    if a is None:
                        return
                    wait(pool, times_cs, a, 2)
                    wait(pool, kturn, a - 1, 1)
                    for i in range(2):
                        nc.gpsimd.tensor_tensor(kv2[:, :, i * DC:(i + 1) * DC], byc[:], bys[:], ALU.add).then_inc(roped2.sem, 1)
                    wait(pool, pair, a - 2, NPAIR - 1)
                    nc.gpsimd.tensor_tensor(kv[par][:], byc[:], bys[:], ALU.add).then_inc(roped.sem, 1)
                    if not (isinstance(a, int) and a == NB - 1):
                        products(a + 1, 1 - par, ha + par)

                pipelined(pool, body)

            @block.tensor
            def _(pe):
                for c in (kturn, unit, sturn, scored, pair, proj):
                    c.start(pe)
                pe.wait_ge(ones_set, 1)

                def turn_keys(a, par, i):
                    if i == 0:
                        wait(pe, roped2, a, 1)
                        wait(pe, uexp, a - 1, NU - 1)
                    else:
                        wait(pe, srow, a - 1)
                    for j in range(6):
                        t = 6 * i + j
                        m = key_rows(t)
                        last = nc.tensor.transpose(key_banks(i)[:, j * 128:j * 128 + m],
                                                   kv2[0:m, t, :], k.ident[0:m, 0:m])
                    last.then_inc(kturn.sem, 1)

                def score_unit(a, par, ha, i):
                    t, m, n0 = i // PARTS, unit_rows(i), 128 * (i // PARTS)
                    first, n = unit_keys(i)
                    if i % PARTS == 0:
                        for c in range(NCH):
                            if (t == 0 and c == 0) or (t and (n0 - 1) // CH < c <= (n0 + m - 1) // CH):
                                wait(pe, q_in[par][c], ha)
                    if i < UB:
                        wait(pe, klow, a, 1)
                    else:
                        wait(pe, uexp, a, i - UB)
                    nc.tensor.matmul(unit_tile(i), qA[par][:, n0:n0 + m], kHH[par][:, first:first + n], start=True, stop=False)
                    nc.tensor.matmul(unit_tile(i), qH[par][0:DC, n0:n0 + m], kL[par][0:DC, first:first + n],
                                     start=False, stop=True).then_inc(unit.sem, 1)

                def turn_shift(a, par):
                    wait(pe, chain_v, a, CHAIN_STEPS - 1)
                    nc.tensor.transpose(P[0:2 * NT, SHIFT_BANK, 0:128], shs[:].rearrange("p l t -> p (l t)").bitcast(F32),
                                        k.ident[:]).then_inc(sturn.sem, 1)

                def scores_t(b, par, hb, s):
                    c, t = slot_work(s)
                    m = key_rows(t)
                    if s == 0:
                        wait(pe, shift_in[par], hb)
                        wait(pe, roped, b)
                    if s < 2:
                        wait(pe, exped, b - 1, s + NSLOT - 2)
                    else:
                        wait(pe, exped, b, s - 2)
                    out, cols, keys = P[0:m, 4 + s % 2, 0:CH], slice(c * CH, (c + 1) * CH), slice(t * 128, t * 128 + m)
                    nc.tensor.matmul(out, kHH[par][:, keys], qA[par][:, cols], start=True, stop=False)
                    nc.tensor.matmul(out, kL[par][:, keys], qH[par][:, cols], start=False, stop=True).then_inc(scored.sem, 1)

                def times_kv(b, par, j):
                    i, t = j // NKT, j % NKT
                    wait(pe, exped, b, 2 * j + 1)
                    if t == 0:
                        if i == 0:
                            wait(pe, cc_ready, b - 1, 1)
                        else:
                            wait(pe, added, b - 1)
                    for up in range(2):
                        last = nc.tensor.matmul(P[64 * up:64 * up + 64, out_bank(par, i), 0:CH], kv[par][:, t, :],
                                                pt[j % 3][:, up, :], start=(t == 0), stop=(t == NKT - 1))
                    last.then_inc(pair.sem, 1)

                def project(b, par, part=None):
                    pairs = range(NH // 2) if part is None else range(2 * part, 2 * part + 2)
                    if pairs[0] == 0:
                        wait(pe, cc_ready, b, 1)
                    for h in pairs:
                        last = nc.tensor.matmul(P[0:SQ, out_bank(par, 2), 0:D], cc[:, h * SQ:(h + 1) * SQ], v1[:, h, :],
                                                start=(h == 0), stop=(h == NH // 2 - 1))
                    if pairs[-1] == NH // 2 - 1:
                        last.then_inc(proj.sem, 1)

                def body(a, b, par, ha, hb):
                    if a is not None:
                        turn_keys(a, par, 0)
                        turn_keys(a, par, 1)
                    for s in range(-PRE, NSLOT):
                        if s < 0 and b is not None and not (isinstance(b, int) and b == 0):
                            project(b - 1, par, s + PRE)
                        if s >= 0 and b is not None:
                            scores_t(b, 1 - par, hb, s)
                        if a is not None:
                            for i in unit_slots.get(s, []):
                                score_unit(a, par, ha, i)
                            if s == CHAIN + TURN_SHIFT:
                                turn_shift(a, par)
                        if b is not None:
                            if s >= 3 and s % 2:
                                times_kv(b, 1 - par, (s - 3) // 2)
                    if b is not None:
                        times_kv(b, 1 - par, NPAIR - 1)
                        if a is None:
                            project(b, 1 - par)

                pipelined(pe, body, heads=2)

            @block.scalar
            def _(act):
                for c in (khigh, uexp, chain_a, exped):
                    c.start(act)

                def high_keys(a, par, i):
                    n = 128 * 5 + key_rows(6 * i + 5)
                    wait(act, kturn, a, i)
                    wait(act, scored, a - 2, NSLOT - 1)
                    nc.scalar.copy(kHH[par][:, 768 * i:768 * i + n], key_banks(i)[:, 0:n]).then_inc(khigh.sem, 1)

                def exp_unit(a, par, i):
                    wait(act, umax, a, i)
                    if i == 0:
                        wait(act, chain_v, a - 1, CHAIN_STEPS - 1)
                    nc.scalar.activation(unit_tile(i), unit_tile(i), ACT.Exp, bias=of_unit(nmax, i),
                                         accum_out=of_unit(den, i)).then_inc(uexp.sem, 1)

                def exp_slot(b, s):
                    j, m = s // 2, key_rows(slot_work(s)[1])
                    wait(act, scored, b, s)
                    if s % 2 == 0:
                        if j < 3:
                            wait(act, pair, b - 1, j - 3 + NPAIR)
                        else:
                            wait(act, pair, b, j - 3)
                    nc.scalar.activation(pt[j % 3][0:m, s % 2, :], P[0:m, 4 + s % 2, 0:CH], ACT.Exp).then_inc(exped.sem, 1)

                def body(a, b, par, ha, hb):
                    if a is not None:
                        high_keys(a, par, 0)
                        high_keys(a, par, 1)
                    for s in range(-PRE, NSLOT):
                        if s >= 0 and b is not None:
                            exp_slot(b, s)
                        if a is not None:
                            for i in unit_slots.get(s - 1, []):
                                exp_unit(a, par, i)
                            if s == CHAIN + 1:
                                wait(act, chain_v, a, 1)
                                nc.scalar.activation(egap[:], gap[:], ACT.Exp).then_inc(chain_a.sem, 1)
                            if s == CHAIN + 3:
                                wait(act, chain_v, a, 5)
                                nc.scalar.activation(part[:], log0[:], ACT.Exp, scale=-1.0).then_inc(chain_a.sem, 1)

                pipelined(act, body, heads=2)

            @block.vector
            def _(dve):
                for c in (klow, umax, chain_v, srow, cc_ready, added):
                    c.start(dve)
                for i in range(2):
                    nc.vector.memset(kL[i][DC:DC + 2, :].bitcast(F32), 1.0)
                nc.vector.memset(nmax[:], 0.0)
                nc.vector.memset(den[:], 1.0)
                nc.vector.drain().then_inc(ones_set, 1)
                dve.wait_ge(ones_set, 1)

                def low_keys(a, par, i):
                    n = 128 * 5 + key_rows(6 * i + 5)
                    wait(dve, khigh, a, i)
                    nc.vector.tensor_tensor(kL[par][0:DC, 768 * i:768 * i + n], key_banks(i)[0:DC, 0:n],
                                            kHH[par][0:DC, 768 * i:768 * i + n].bitcast(F32), ALU.subtract).then_inc(klow.sem, 1)

                def max_unit(a, par, i):
                    wait(dve, unit, a, i)
                    if i == 0:
                        wait(dve, chain_v, a - 1, CHAIN_STEPS - 1)
                        wait(dve, uexp, a - 1, NU - 1)
                    nc.vector.tensor_reduce(of_unit(nmax, i), unit_tile(i), AX.X, ALU.max, negate=True).then_inc(umax.sem, 1)

                def every(tile):
                    return tile[:].rearrange("p (t o) -> p t o", o=1).to_broadcast([128, NT, PARTS])

                def chain_1(a):
                    wait(dve, umax, a, NU - 1)
                    wait(dve, chain_v, a - 1, CHAIN_STEPS - 1)
                    nc.vector.tensor_reduce(nm[:], nmax[:], AX.X, ALU.min).then_inc(chain_v.sem, 1)
                    wait(dve, chain_v, a, 0)
                    nc.vector.tensor_tensor(gap[:], every(nm), nmax[:], ALU.subtract).then_inc(chain_v.sem, 1)

                def link(a, i, ins):
                    ins.then_inc(chain_v.sem, 1)
                    wait(dve, chain_v, a, i)

                def chain_2(a):
                    wait(dve, chain_a, a, 0)
                    wait(dve, uexp, a, NU - 1)
                    link(a, 2, nc.vector.tensor_tensor(egap[:], egap[:], den[:], ALU.mult))
                    link(a, 3, nc.vector.tensor_reduce(total[:], egap[:], AX.X, ALU.add))
                    link(a, 4, nc.vector.tensor_copy(log0[:], total[:].bitcast(mybir.dt.int32)))
                    link(a, 5, nc.vector.tensor_scalar(log0[:], log0[:], LN2 / 2 ** 23, -(127 - 0.043) * LN2, ALU.mult, ALU.add))
                    link(a, 6, nc.vector.tensor_tensor(shift[:], nm[:], log0[:], ALU.subtract))

                def chain_3(a):
                    wait(dve, chain_a, a, 1)
                    link(a, 7, nc.vector.tensor_tensor(delta[:], total[:], part[:], ALU.mult))
                    link(a, 8, nc.vector.tensor_scalar(delta[:], delta[:], -1.0, None, ALU.add))
                    link(a, 9, nc.vector.tensor_scalar(series[:], delta[:], -0.25, None, ALU.mult))
                    for i, c in ((10, 1 / 3), (11, -0.5), (12, 1.0)):
                        link(a, i, nc.vector.scalar_tensor_tensor(out=series[:], in0=series[:], scalar=c, in1=delta[:],
                                                                  op0=ALU.add, op1=ALU.mult))
                    link(a, 13, nc.vector.tensor_tensor(shift[:], shift[:], series[:], ALU.subtract))
                    wait(dve, sturn, a - 1)
                    link(a, 14, nc.vector.tensor_copy(shs[:, 0, :], shift[:]))
                    nc.vector.tensor_tensor(shs[:, 1, :], shift[:], shs[:, 0, :].bitcast(F32), ALU.subtract).then_inc(chain_v.sem, 1)

                def row_of_shift(a, par, ha):
                    wait(dve, sturn, a)
                    if not (isinstance(a, int) and a == 0):
                        wait(dve, shift_out[1 - par], ha - 1 + par)
                    nc.vector.tensor_copy(rows[:], P[0:2 * NT, SHIFT_BANK, 0:128]).then_inc(srow.sem, 1)

                def keep(b, par, i):
                    wait(dve, pair, b, (i + 1) * NKT - 1)
                    wait(dve, proj, b - 1)
                    nc.vector.tensor_copy(cc[:, i * CH:(i + 1) * CH], P[:, out_bank(par, i), 0:CH]).then_inc(cc_ready.sem, 1)

                def add(b, par):
                    wait(dve, proj, b)
                    xb = k.x[:, ds(b, 1), :].rearrange("q o d -> q (o d)")
                    nc.vector.scalar_tensor_tensor(out=xb, in0=P[0:SQ, out_bank(par, 2), 0:D], scalar=k.gates[0:SQ, 1:2], in1=xb,
                                                   op0=ALU.mult, op1=ALU.add).then_inc(added.sem, 1)

                def body(a, b, par, ha, hb):
                    if a is not None:
                        low_keys(a, par, 0)
                        low_keys(a, par, 1)
                    for s in range(-PRE, NSLOT):
                        if s == 0 and b is not None and not (isinstance(b, int) and b == 0):
                            add(b - 1, par)
                        if a is not None:
                            for i in unit_slots.get(s, []):
                                max_unit(a, par, i)
                            for n, step in ((0, chain_1), (2, chain_2), (4, chain_3)):
                                if s == CHAIN + n:
                                    step(a)
                            if s == CHAIN + TURN_SHIFT + 1:
                                row_of_shift(a, par, ha)
                        if b is not None:
                            if s == 2 * NKT + 3:
                                keep(b, 1 - par, 0)
                    if b is not None:
                        keep(b, 1 - par, 1)
                        if a is None:
                            add(b, 1 - par)

                pipelined(dve, body, heads=2)


def layer_1(k):
    with ExitStack() as st:
        v1 = k.sbuf("v1", [128, NH // 2, D], F32, st)
        with ExitStack() as inner:
            wa = [k.sbuf(f"wb{x}", [128, KT, NH * DCQ], F32R, inner) for x in "HL"]
            mm = k.sbuf("mm", [HALF, 2, NH * DC], F32, inner)
            prepare_1(k, wa, mm, v1)
            queries_1(k, wa, mm)
        attention_1(k, v1)



def build(nc, dram, stop=99):
    with ExitStack() as stack:
        k = Core(nc, dram, stack)
        with ExitStack() as st:
            wa = [k.sbuf(f"wa{x}", [128, KT, NH * DC], F32R, st) for x in "HL"]
            v0 = k.sbuf("v0", [128, NH // 2, D], F32, st)
            maskq = k.sbuf("maskq", [SQ, SQ], BF16, st)
            identb = k.sbuf("identb", [128, 128], BF16, st)
            prepare_0(k, wa, v0, maskq, identb)
            if stop >= 1:
                layer_norm(k, 0)
                queries_0(k, wa)
            if stop >= 2:
                attention_0(k, v0, maskq, identb)
        if stop >= 3:
            layer_norm(k, 1)
            route(k, 0, 32, 8, 4, 8, dram["router0"], dram["bias0"], False, 0.0)
        if stop >= 4:
            experts(k, 0, 32, dram["experts0"], 2)
            k.clear_semaphores()
        if stop >= 5:
            layer_norm(k, 2)
            layer_1(k)
        if stop >= 6:
            layer_norm(k, 3)
            route(k, 1, 16, 4, 2, 4, dram["router1"], dram["bias1"], True, 1e-20)
            experts(k, 1, 16, dram["experts1"], 3)
        with nc.semaphore("out_stored") as stored, nc.Block() as block:
            @block.sync
            def _(sp):
                sp.dma_start(dram["out"].rearrange("b q d -> q b d"), k.x[:]).then_inc(stored, 16)
                sp.wait_ge(stored, 16)


def lay_out(v):
    f = {n: np.asarray(a) for n, a in v.items()}

    def heads(w):
        return w.reshape(NH, -1, w.shape[-1]).transpose(1, 0, 2)

    def tiles(w):
        return w.reshape(KT, 128, -1).transpose(1, 0, 2).reshape(128, -1)

    def packed(gate, up, down, sg, su, sd):
        rows = [np.concatenate([tiles(g), tiles(u), d], 1) for g, u, d in zip(gate, up, down)]
        for i in range(2):
            c = slice(i * FF, (i + 1) * FF)
            rows.append(np.concatenate([tiles(sg[:, c]), tiles(su[:, c]), sd[c]], 1))
        return np.stack(rows)

    kv = f["L0_xattn_Wkv_expand"]
    out = {
        "x": f["x"], "ctx": f["ctx_512"], "g_xattn": f["g_xattn"], "g_ffn": f["g_ffn"],
        "w_attn0": np.concatenate([heads(f["L0_xattn_Wq"]), heads(kv[:D]), heads(kv[D:]), heads(f["L0_xattn_Wout"].T)], 2),
        "router0": f["L0_ffn_router_w"].reshape(KT, 128, 32).transpose(1, 0, 2), "bias0": f["L0_ffn_router_bias"],
        "experts0": packed(*(f["L0_ffn_" + n] for n in ("w_gate", "w_up", "w_down", "sw_gate", "sw_up", "sw_down"))),
        "wqk1": np.concatenate([f["L1_xattn_Wq"].reshape(NH, 128, D).transpose(1, 0, 2),
                                f["L1_xattn_w_kc_q"].transpose(1, 0, 2)], 2),
        "wvo1": np.concatenate([f["L1_xattn_w_kc_kv"].transpose(1, 0, 2),
                                f["L1_xattn_Wo"].T.reshape(NH, 128, D).transpose(1, 0, 2)], 2),
        "wr1": np.concatenate([f["L1_xattn_W_qr"].transpose(2, 0, 1), f["L1_xattn_W_kr"].transpose(2, 0, 1)], 2),
        "router1": f["L1_ffn_gate_weight"].T.reshape(KT, 128, 16).transpose(1, 0, 2),
        "bias1": f["L1_ffn_e_score_correction_bias"],
        "experts1": packed(*(f["L1_ffn_" + n].swapaxes(-1, -2) for n in ("gate_w", "up_w", "down_w")),
                           *(f["L1_ffn_" + n].T for n in ("sh_gate_w", "sh_up_w", "sh_down_w"))),
        "ident": np.eye(128, dtype=np.float32), "ident_bf16": np.eye(128).astype(mybir.dt.np(BF16)),
        "mask": np.where(np.tril(np.ones((SQ, SQ), bool)), 0, LOWEST).astype(mybir.dt.np(BF16)),
    }
    for n in (8, 4):
        out[f"earlier{n}"] = np.tril(np.ones((n, n), np.float32), -1)

    def rope(length, width):
        inv = np.float32(1.0) / np.float32(10000.0) ** (np.arange(0, width, 2, dtype=np.float32) / np.float32(width))
        angle = np.arange(length, dtype=np.float32)[:, None] * inv[None, :]
        return np.repeat(np.cos(angle), 2, -1), np.repeat(np.sin(angle), 2, -1)

    cos, sin = (t.T.reshape(2, HALF, SQ) for t in rope(SQ, DCQ))
    out["rope_q"] = np.stack([np.stack([cos[0], sin[1]], 1), np.stack([sin[0], cos[1]], 1)], 1)
    cos, sin = (np.pad(t, ((0, NKT * 128 - SK), (0, 0))).reshape(NKT, 128, DC).transpose(1, 0, 2) for t in rope(SK, DC))
    half = np.where(np.arange(DC) < DC // 2, np.float32(-1), np.float32(1))
    out["rope_k"] = np.stack([cos, sin * half], 1)
    return {n: np.ascontiguousarray(a) for n, a in out.items()}


def kernel(**inputs):
    import concourse.bacc as bacc
    from concourse.bass_utils import run_bass_kernel_spmd

    arrays = lay_out(inputs)
    nc = bacc.Bacc("TRN2", target_bir_lowering=False, num_devices=1)
    dram = {n: nc.dram_tensor("in_" + n, a.shape, mybir.dt.from_np(a.dtype), kind="ExternalInput").ap() for n, a in arrays.items()}
    dram["out"] = nc.dram_tensor("out", [NB, SQ, D], F32, kind="ExternalOutput").ap()
    dram["q_lat"] = nc.dram_tensor("q_lat", [NB, 2, DC, NH, SQ], F32).ap()
    dram["shift"] = nc.dram_tensor("shift", [2, 2, 13 * 128], F32).ap()
    dram["route"] = nc.dram_tensor("route", [34, T], F32).ap()
    build(nc, dram)
    result = run_bass_kernel_spmd(nc, [{"in_" + n: a for n, a in arrays.items()}], core_ids=[0])
    return result.results[0]["out"]
```

```python
from contextlib import ExitStack
import math

import concourse.bass as bass
from concourse import mybir
import numpy as np

F32 = mybir.dt.float32
F32R = mybir.dt.float32r
BF16 = mybir.dt.bfloat16
ALU = mybir.AluOpType
ACT = mybir.ActivationFunctionType
AX = mybir.AxisListType

NB, SQ, D = 16, 100, 256
T = NB * SQ
NH = 16
SK, DC = 1444, 64
KT = D // 128
NKT = (SK + 127) // 128
KREST = SK - (NKT - 1) * 128
HQ = NH * SQ
CH = 4 * SQ
NCH = HQ // CH
DCQ, HALF = 192, 96
FF = 128
EPS = 1e-5
LN2 = math.log(2)
LOWEST = -3.0e38
HIGHEST, CHOSEN = 3.0e38, 2.0e38


def ds(start, n):
    return bass.ds(start, n)


class Core:

    def __init__(self, nc, dram, stack):
        self.nc, self.dram, self.stack = nc, dram, stack
        self.used = []
        self.psum = stack.enter_context(nc.psum_tensor("psum", [128, 8, 512], F32))
        self.x = self.sbuf("x_sb", [SQ, NB, D], F32)
        self.xnH = self.sbuf("xnH", [128, KT, T], F32R)
        self.xnL = self.sbuf("xnL", [128, KT, T], F32R)
        self.ident = self.sbuf("ident", [128, 128], F32)
        self.gates = self.sbuf("gates", [128, 4], F32)
        self.stats = self.sbuf("ln_stats", [SQ, NB, 6], F32)
        self.stat_s = [self.sem(stack, f"ln{i}_stat") for i in range(4)]
        self.early = [[], [], [], []]

    def sbuf(self, name, shape, dtype, stack=None):
        return (stack or self.stack).enter_context(self.nc.sbuf_tensor(name, shape, dtype))

    def sem(self, stack, name):
        handle = stack.enter_context(self.nc.semaphore(name))
        self.used.append(handle.num)
        return handle

    def gather(self, dve, tag, b):
        self.nc.vector.bn_stats(self.stats[:, b, :], self.x[:, b, :]).then_inc(self.stat_s[tag], 1)
        self.early[tag].append(b)

    def clear_semaphores(self):
        with self.nc.Block() as block:
            @block.sync
            def _(sp):
                sp.sem_clear(range(min(self.used), max(self.used) + 1))
        self.used = []


class Stage:

    def __init__(self, sync=None, tensor=None, scalar=None, vector=None, gpsimd=None):
        self.sync, self.tensor, self.scalar, self.vector, self.gpsimd = sync, tensor, scalar, vector, gpsimd


def together(k, *stages):
    with k.nc.Block() as block:
        @block.sync
        def _(sp):
            for s in stages:
                if s.sync:
                    s.sync(sp)

        @block.tensor
        def _(pe):
            for s in stages:
                if s.tensor:
                    s.tensor(pe)

        @block.scalar
        def _(act):
            for s in stages:
                if s.scalar:
                    s.scalar(act)

        @block.vector
        def _(dve):
            for s in stages:
                if s.vector:
                    s.vector(dve)

        @block.gpsimd
        def _(pool):
            for s in stages:
                if s.gpsimd:
                    s.gpsimd(pool)



def prepare_0(k, wa, v0, maskq, identb, st):
    nc, P = k.nc, k.psum
    waH, waL = wa
    w = k.sbuf("w_attn0", [16, NH, 640], F32, st)
    graw = k.sbuf("graw", [128, 4], F32, st)
    loaded, x_loaded = k.sem(st, "p0_loaded"), k.sem(st, "p0_x_loaded")
    qk_done, vo_done, high_done, low_done = (k.sem(st, f"p0_{n}") for n in ("qk", "vo", "high", "low"))
    def sync(sp):
        sp.dma_start(w[:], k.dram["w_attn0"]).then_inc(loaded, 16)
        sp.dma_start(k.x[:], k.dram["x"].rearrange("b q d -> q b d")).then_inc(x_loaded, 16)
        sp.dma_start(k.ident[:], k.dram["ident"]).then_inc(loaded, 16)
        sp.dma_start(graw[:, 0:2], k.dram["g_xattn"].partition_broadcast(128)).then_inc(loaded, 16)
        sp.dma_start(graw[:, 2:4], k.dram["g_ffn"].partition_broadcast(128)).then_inc(loaded, 16)
        sp.dma_start(maskq[:], k.dram["mask"]).then_inc(loaded, 16)
        sp.dma_start(identb[:], k.dram["ident_bf16"]).then_inc(loaded, 16)

    def tensor(pe):
        pe.wait_ge(loaded, 96)
        for h in range(NH):
            for kt in range(KT):
                last = nc.tensor.matmul(P[:, 2 * kt + h % 8 // 4, (2 * (h % 4) + h // 8) * DC:(2 * (h % 4) + h // 8 + 1) * DC],
                                        w[:, h, kt * 128:(kt + 1) * 128], w[:, h, 256:320],
                                        start=True, stop=True)
        last.then_inc(qk_done, 1)
        for h in range(NH):
            pair, up = 4 * (h // 8) + h % 4, (h // 4) % 2
            last = nc.tensor.matmul(P[64 * up:64 * up + 64, 4 + pair // 2, (pair % 2) * D:(pair % 2 + 1) * D],
                                    w[:, h, 320:384], w[:, h, 384:640], start=True, stop=True)
        last.then_inc(vo_done, 1)

    def scalar(act):
        act.wait_ge(loaded, 96)
        nc.scalar.activation(k.gates[:], graw[:], ACT.Tanh)
        act.wait_ge(qk_done, 1)
        nc.scalar.activation(waH[:].rearrange("p t n -> p (t n)"),
                             P[:, 0:4, :].rearrange("p b n -> p (b n)"), ACT.Copy, scale=0.25).then_inc(high_done, 1)
        act.wait_ge(vo_done, 1)
        nc.scalar.copy(v0[:].rearrange("p t n -> p (t n)"), P[:, 4:8, :].rearrange("p b n -> p (b n)"))

    def vector(dve):
        dve.wait_ge(high_done, 1)
        nc.vector.scalar_tensor_tensor(out=waL[:].rearrange("p t n -> p (t n)"),
                                       in0=P[:, 0:4, :].rearrange("p b n -> p (b n)"), scalar=0.25,
                                       in1=waH[:].rearrange("p t n -> p (t n)").bitcast(F32),
                                       op0=ALU.mult, op1=ALU.subtract).then_inc(low_done, 1)
    return Stage(sync=sync, tensor=tensor), scalar, vector, (x_loaded, 16), (low_done, 1)



def layer_norm(k, tag, st, ready=None, free=None, between_dve=None, between_act=None, bank0=0):
    nc, P = k.nc, k.psum
    GRP = 2
    mv = k.sbuf(f"ln_mv{tag}", [SQ, NB, 2], F32, st)
    std = k.sbuf(f"ln_std{tag}", [SQ, NB], F32, st)
    rstd = k.sbuf(f"ln_rstd{tag}", [SQ, NB], F32, st)
    shift = k.sbuf(f"ln_shift{tag}", [SQ, NB], F32, st)
    eps = k.sbuf(f"ln_eps{tag}", [SQ, 1], F32, st)
    xn = k.sbuf(f"ln_xn{tag}", [SQ, NB, D], F32, st)
    stats, stat_s, early = k.stats, k.stat_s[tag], k.early[tag]
    eps_s, var_s, std_s, rstd_s, norm_s, turn_s, high_s, low_s, shift_s, norm2_s = (
        k.sem(st, f"ln{tag}_{n}") for n in ("eps", "var", "std", "rstd", "norm", "turned", "high", "low", "shift", "norm2"))
    def vector(dve):
        nc.vector.memset(eps[:], EPS).then_inc(eps_s, 1)
        if ready:
            dve.wait_ge(*ready)
        late = [b for b in range(NB) if b not in early]
        for b in late:
            nc.vector.bn_stats(stats[:, b, :], k.x[:, b, :]).then_inc(stat_s, 1)
        for i, b in enumerate(early + late):
            dve.wait_ge(stat_s, i + 1)
            nc.vector.bn_aggr(mv[:, b, :], stats[:, b, :]).then_inc(var_s, 1)
        dve.wait_ge(std_s, 1)
        nc.vector.reciprocal(rstd[:], std[:]).then_inc(rstd_s, 1)
        dve.wait_ge(rstd_s, 1)
        dve.wait_ge(var_s, NB)
        nc.vector.scalar_tensor_tensor(out=shift[:], in0=mv[:, :, 0], scalar=-1.0, in1=rstd[:],
                                       op0=ALU.mult, op1=ALU.mult).then_inc(shift_s, 1)
        for b in range(0, NB, 2):
            nc.vector.tensor_scalar(xn[:, b, :], k.x[:, b, :], mv[:, b, 0:1], rstd[:, b:b + 1],
                                    ALU.subtract, ALU.mult).then_inc(norm_s, 1)
        if between_dve:
            between_dve(dve)
        with dve.Fori(0, NB // GRP // 4) as j:
            for g in range(4):
                dve.wait_ge(high_s, 4 * j + g + 1)
                low = k.xnL[:, :, ds(j * 4 * GRP * SQ + g * GRP * SQ, GRP * SQ)]
                high = k.xnH[:, :, ds(j * 4 * GRP * SQ + g * GRP * SQ, GRP * SQ)]
                nc.vector.tensor_tensor(low, P[:, bank0 + g, 0:KT * GRP * SQ].rearrange("p (t n) -> p t n", t=KT),
                                        high.bitcast(F32), ALU.subtract).then_inc(low_s, 1)

    def scalar(act):
        act.wait_ge(var_s, NB)
        act.wait_ge(eps_s, 1)
        nc.scalar.activation(std[:], mv[:, :, 1], ACT.Sqrt, bias=eps[:, 0:1]).then_inc(std_s, 1)
        act.wait_ge(shift_s, 1)
        for b in range(1, NB, 2):
            nc.scalar.activation(xn[:, b, :], k.x[:, b, :], ACT.Identity, scale=rstd[:, b:b + 1], bias=shift[:, b:b + 1]
                                 ).then_inc(norm2_s, 1)
        if between_act:
            between_act(act)
        with act.Fori(0, NB // GRP // 4) as j:
            for g in range(4):
                act.wait_ge(turn_s, 4 * j + g + 1)
                nc.scalar.copy(k.xnH[:, :, ds(j * 4 * GRP * SQ + g * GRP * SQ, GRP * SQ)],
                               P[:, bank0 + g, 0:KT * GRP * SQ].rearrange("p (t n) -> p t n", t=KT)).then_inc(high_s, 1)

    def tensor(pe):
        if free:
            pe.wait_ge(*free)
        for g in range(NB // GRP):
            pe.wait_ge(norm_s, g + 1)
            pe.wait_ge(norm2_s, g + 1)
            if g >= 4:
                pe.wait_ge(low_s, g - 3)
            for kt in range(KT):
                for i in range(GRP):
                    c = (kt * GRP + i) * SQ
                    last = nc.tensor.transpose(P[:, bank0 + g % 4, c:c + SQ],
                                               xn[:, GRP * g + i, kt * 128:(kt + 1) * 128],
                                               k.ident[0:SQ, 0:SQ])
            last.then_inc(turn_s, 1)
    return Stage(vector=vector, scalar=scalar, tensor=tensor), (low_s, NB // GRP)



def queries_0(k, wa, st):
    nc, P = k.nc, k.psum
    waH, waL = wa
    NPR, BUF = NH // 2, 4
    qs = [k.sbuf(f"q0_out{i}", [128, 4, 2, 4, SQ], F32R, st) for i in range(2)]
    prod_s, high_s, low_s = (k.sem(st, f"q0_{n}") for n in ("prod", "high", "low"))
    stored = [k.sem(st, f"q0_stored{i}") for i in range(2)]
    def tensor(pe):
        pe.sem_inc(low_s, BUF)
        with pe.Fori(0, NCH) as c:
            for p in range(NPR):
                pe.wait_ge(low_s, NPR * c + p + 1)
                for kt in range(KT):
                    wH, wL = (w[:, kt, p * 128:(p + 1) * 128] for w in (waH, waL))
                    xH, xL = (x[:, kt, ds(c * CH, CH)] for x in (k.xnH, k.xnL))
                    out = P[:, p % BUF, 0:CH]
                    nc.tensor.matmul(out, wH, xH, start=(kt == 0), stop=False)
                    nc.tensor.matmul(out, wH, xL, start=False, stop=False)
                    last = nc.tensor.matmul(out, wL, xH, start=False, stop=(kt == KT - 1))
                last.then_inc(prod_s, 1)
        pe.wait_ge(low_s, BUF + NPR * NCH)

    def scalar(act):
        for i in range(2):
            act.sem_inc(stored[i], 32)
        with act.Fori(0, NCH) as c:
            for p in range(NPR):
                act.wait_ge(prod_s, NPR * c + p + 1)
                if p % 4 == 0:
                    act.wait_ge(stored[p // 4], 32 * c + 32)
                nc.scalar.copy(qs[p // 4][:, :, 0, p % 4, :], by_sequence(P[:, p % BUF, 0:CH])).then_inc(high_s, 1)

    def vector(dve):
        with dve.Fori(0, NCH) as c:
            for p in range(NPR):
                dve.wait_ge(high_s, NPR * c + p + 1)
                nc.vector.tensor_tensor(qs[p // 4][:, :, 1, p % 4, :], by_sequence(P[:, p % BUF, 0:CH]),
                                        qs[p // 4][:, :, 0, p % 4, :].bitcast(F32), ALU.subtract).then_inc(low_s, 1)

    def store(sp, c):
        for i in range(2):
            sp.wait_ge(low_s, NPR * c + 4 * i + 4 + BUF)
            store_queries(k, sp, qs[i], c, i, stored[i])

    def sync_first(sp):
        with sp.Fori(0, NCH - 1) as c:
            store(sp, c)

    def chunks_stored(sp, n):
        for i in range(2):
            sp.wait_ge(stored[i], 32 + 32 * n)

    return Stage(sync=sync_first), Stage(sync=lambda sp: store(sp, NCH - 1), tensor=tensor, scalar=scalar, vector=vector), chunks_stored


def by_sequence(tile):
    return tile.rearrange("p (b q) -> p b q", b=4)


def store_queries(k, sp, qs, c, quad, stored):
    for hh in range(2):
        h0 = 8 * hh + 4 * quad
        sp.dma_start(k.dram["q_lat"][ds(4 * c, 4), :, :, h0:h0 + 4, :].rearrange("b l d h q -> d (b l) (h q)"),
                     qs[64 * hh:64 * hh + 64].rearrange("p b l h q -> p (b l) (h q)").bitcast(F32)).then_inc(stored, 16)


class Count:

    AHEAD = 2

    def __init__(self, k, stack, name, per, unit=1):
        self.sem, self.per, self.unit = k.sem(stack, name), per, unit

    def start(self, eng):
        eng.sem_inc(self.sem, self.AHEAD * self.per * self.unit)

    def upto(self, b, i=0):
        return (b + self.AHEAD) * (self.per * self.unit) + (i + 1) * self.unit


def wait(eng, count, b, i=0):
    eng.wait_ge(count.sem, count.upto(b, i))


def pipelined(eng, body, heads=1, peel_last=False):
    body(0, None, 0, 0, None)
    if heads == 2:
        body(1, 0, 1, 0, 0)
        with eng.Fori(0, NB // 2 - 1 - peel_last) as j:
            body(2 * j + 2, 2 * j + 1, 0, j + 1, j)
            body(2 * j + 3, 2 * j + 2, 1, j + 1, j + 1)
        if peel_last:
            body(NB - 2, NB - 3, 0, NB // 2 - 1, NB // 2 - 2)
            body(NB - 1, NB - 2, 1, NB // 2 - 1, NB // 2 - 1)
        body(None, NB - 1, 0, None, NB // 2 - 1)
        return
    with eng.Fori(0, (NB - 2) // 2) as j:
        body(2 * j + 1, 2 * j, 1, j, j)
        body(2 * j + 2, 2 * j + 1, 0, j + 1, j)
    body(NB - 1, NB - 2, 1, NB // 2 - 1, NB // 2 - 1)
    body(None, NB - 1, 0, None, NB // 2 - 1)



def attention_0(k, v0, maskq, identb, chunks_stored, st):
    nc, P = k.nc, k.psum
    ctx = [k.sbuf(f"a0_ctx{i}", [SQ, DC], F32, st) for i in range(2)]
    ctx2 = [k.sbuf(f"a0_ctx2{i}", [SQ, 2, DC], F32, st) for i in range(2)]
    qA = [k.sbuf(f"a0_qA{i}", [128, HQ], F32R, st) for i in range(2)]
    kHH = k.sbuf("a0_kHH", [128, SQ], F32R, st)
    kL = k.sbuf("a0_kL", [DC, SQ], F32R, st)
    mx = k.sbuf("a0_max", [SQ, NH], F32, st)
    den = k.sbuf("a0_den", [SQ, NH], F32, st)
    rden = k.sbuf("a0_rden", [SQ, NH], F32, st)
    e = [k.sbuf(f"a0_e{i}", [SQ, NH, SQ], F32, st) for i in range(2)]
    pt = [k.sbuf(f"a0_pt{i}", [SQ, CH], F32, st) for i in range(4)]
    cc = k.sbuf("a0_cc", [128, 2, CH], F32, st)

    def count(name, per, unit=1):
        return Count(k, st, f"a0_{name}", per, unit)

    ctx_in = [count(f"ctx_in{i}", 1, 16) for i in range(2)]
    ctx2_in = [count(f"ctx2_in{i}", 1, 32) for i in range(2)]
    q_in = [count(f"q_in{i}", 1, 16) for i in range(2)]
    kturn, khigh, klow = count("kturn", 1), count("khigh", 1), count("klow", 1)
    score, maxed, shifted = count("score", 2), count("maxed", 2), count("shifted", 2)
    exped, summed, inverse, prob = count("exped", 2), count("summed", 2), count("inverse", 1), count("prob", 2)
    turned, pt_ready, pv, cc_ready = count("turned", 4), count("pt_ready", 4), count("pv", 2), count("cc_ready", 2)
    proj, added = count("proj", 1), count("added", 1)
    HB = NH // 2

    def follows(a):
        return not (isinstance(a, int) and a == NB - 1)

    def score_banks(half):
        return P[0:SQ, 2 * half:2 * half + 2, 0:CH].rearrange("q b (h s) -> q b h s", h=4)

    def by_bank(tile, half):
        return tile[:, HB * half:HB * half + HB].rearrange("q (b h) -> q b h", b=2)

    def start_loads(sp):
        for c in ctx_in + ctx2_in + q_in:
            c.start(sp)
        chunks_stored(sp, 1)
        load(sp, 0, False)

    def load(sp, j, again):
        for par in range(2):
            a = 2 * j + par
            if again:
                wait(sp, kturn, a - 2)
            for i in range(2):
                sp.dma_start(ctx2[par][:, i, :], k.dram["ctx"][ds(a, 1), 0:SQ, :].rearrange("o s d -> (o s) d")
                             ).then_inc(ctx2_in[par].sem, 16)
            if again:
                wait(sp, score, a - 2, 1)
            sp.dma_start(qA[par][:].bitcast(F32), k.dram["q_lat"][ds(a, 1)].rearrange("o l d h q -> (o l d) (h q)")
                         ).then_inc(q_in[par].sem, 16)
            if again:
                wait(sp, pv, a - 2, 1)
            sp.dma_start(ctx[par][:], k.dram["ctx"][ds(a, 1), 0:SQ, :].rearrange("o s d -> (o s) d")
                         ).then_inc(ctx_in[par].sem, 16)

    def sync(sp):
        chunks_stored(sp, NCH)
        with sp.Fori(1, NB // 2) as j:
            load(sp, j, True)

    def tensor(pe):
        for c in (kturn, score, turned, pv, proj):
            c.start(pe)

        def turn_keys(a, par, half_a):
            wait(pe, ctx2_in[par], half_a)
            if not (isinstance(a, int) and a < 3):
                wait(pe, cc_ready, a - 3, 1)
            nc.tensor.transpose(P[:, 7, 0:SQ], ctx2[par][:].rearrange("s i d -> s (i d)"),
                                k.ident[0:SQ, 0:SQ]).then_inc(kturn.sem, 1)

        def scores(a, par, half_a, half):
            if half == 0:
                wait(pe, q_in[par], half_a)
                wait(pe, khigh, a)
                wait(pe, klow, a)
            wait(pe, shifted, a - 1, half)
            for bank in (2 * half, 2 * half + 1):
                nc.tensor.matmul(P[0:SQ, bank, 0:CH], identb[0:SQ, 0:SQ],
                                 maskq[:].rearrange("q (o s) -> q o s", o=1).to_broadcast([SQ, 4, SQ]),
                                 start=True, stop=True, skip_group_check=True)
                for i in range(4):
                    h = 4 * bank + i
                    out = P[0:SQ, bank, i * SQ:(i + 1) * SQ]
                    nc.tensor.matmul(out, qA[par][:, h * SQ:(h + 1) * SQ], kHH[:], start=False, stop=False,
                                     skip_group_check=True)
                    last = nc.tensor.matmul(out, qA[par][0:DC, h * SQ:(h + 1) * SQ], kL[:], start=False,
                                            stop=True, skip_group_check=True)
            last.then_inc(score.sem, 1)

        def turn_probs(b, par, i):
            wait(pe, prob, b, i // 2)
            if i < 2:
                wait(pe, pt_ready, b - 1, i + 2)
            else:
                wait(pe, pt_ready, b, i - 2)
            for h in range(4):
                last = nc.tensor.transpose(P[0:SQ, 4 + i % 2, h * SQ:(h + 1) * SQ], e[par][:, 4 * i + h, :],
                                           k.ident[0:SQ, 0:SQ])
            last.then_inc(turned.sem, 1)

        def times_ctx(a, b, par, half_b, i):
            wait(pe, pt_ready, b, 2 * i + 1)
            wait(pe, ctx_in[par], half_b)
            if i == 0:
                wait(pe, added, b - 1)
            elif a is None:
                wait(pe, klow, b)
            else:
                wait(pe, klow, a + 1 if follows(a) else a)
            for up in range(2):
                last = nc.tensor.matmul(P[64 * up:64 * up + 64, 6 + i, 0:CH], ctx[par][:], pt[2 * i + up][:],
                                        start=True, stop=True)
            last.then_inc(pv.sem, 1)

        def project(b):
            wait(pe, cc_ready, b, 1)
            for p in range(8):
                last = nc.tensor.matmul(P[0:SQ, 6, 0:D], cc[:, p // 4, (p % 4) * SQ:(p % 4 + 1) * SQ],
                                        v0[:, p, :], start=(p == 0), stop=(p == 7))
            last.then_inc(proj.sem, 1)

        def body(a, b, par, ha, hb):
            if a is not None:
                scores(a, par, ha, 0)
            if b is not None:
                turn_probs(b, 1 - par, 0)
                turn_probs(b, 1 - par, 1)
            if a is not None:
                scores(a, par, ha, 1)
                if follows(a):
                    turn_keys(a + 1, 1 - par, ha + par)
            if b is not None:
                turn_probs(b, 1 - par, 2)
                turn_probs(b, 1 - par, 3)
                if not (isinstance(b, int) and b == 0):
                    project(b - 1)
                times_ctx(a, b, 1 - par, hb, 0)
                times_ctx(a, b, 1 - par, hb, 1)
                if a is None:
                    project(b)

        turn_keys(0, 0, 0)
        pipelined(pe, body, heads=2, peel_last=True)

    def scalar(act):
        for c in (khigh, exped, pt_ready):
            c.start(act)

        def high_keys(a):
            wait(act, kturn, a)
            wait(act, score, a - 1, 1)
            nc.scalar.copy(kHH[:], P[:, 7, 0:SQ]).then_inc(khigh.sem, 1)

        def exp_half(a, par, half):
            wait(act, shifted, a, half)
            tile = e[par][:, HB * half:HB * half + HB, :]
            nc.scalar.activation(tile, tile, ACT.Exp).then_inc(exped.sem, 1)

        def body(a, b, par, ha, hb):
            for half in range(2):
                if b is not None:
                    for i in (2 * half, 2 * half + 1):
                        wait(act, turned, b, i)
                        wait(act, pv, b - 1, i // 2)
                        nc.scalar.copy(pt[i][:], P[0:SQ, 4 + i % 2, 0:CH]).then_inc(pt_ready.sem, 1)
                if a is not None:
                    if half == 0 and follows(a):
                        high_keys(a + 1)
                    exp_half(a, par, half)

        high_keys(0)
        pipelined(act, body, heads=2, peel_last=True)

    def vector(dve):
        for c in (klow, maxed, shifted, summed, inverse, cc_ready, added):
            c.start(dve)

        def shift(a, par, half):
            wait(dve, score, a, half)
            wait(dve, shifted, a - 1, half)
            nc.vector.tensor_reduce(by_bank(mx, half), score_banks(half), AX.X, ALU.max).then_inc(maxed.sem, 1)
            wait(dve, maxed, a, half)
            wait(dve, turned, a - 2, 3)
            nc.vector.tensor_tensor(e[par][:, HB * half:HB * half + HB, :].rearrange("q (b h) s -> q b h s", b=2),
                                    score_banks(half),
                                    by_bank(mx, half).rearrange("q b (h o) -> q b h o", o=1).to_broadcast([SQ, 2, 4, SQ]),
                                    ALU.subtract).then_inc(shifted.sem, 1)

        def keep(b, i):
            wait(dve, pv, b, i)
            wait(dve, proj, b - 1)
            nc.vector.tensor_copy(cc[:, i, :], P[:, 6 + i, 0:CH]).then_inc(cc_ready.sem, 1)

        def low_keys(a):
            wait(dve, khigh, a)
            wait(dve, score, a - 1, 1)
            nc.vector.tensor_tensor(kL[:], P[0:DC, 7, 0:SQ], kHH[0:DC, :].bitcast(F32),
                                    ALU.subtract).then_inc(klow.sem, 1)

        def add(b):
            wait(dve, proj, b)
            xb = k.x[:, ds(b, 1), :].rearrange("q o d -> q (o d)")
            nc.vector.scalar_tensor_tensor(out=xb, in0=P[0:SQ, 6, 0:D], scalar=k.gates[0:SQ, 0:1], in1=xb,
                                           op0=ALU.mult, op1=ALU.add).then_inc(added.sem, 1)

        def body(a, b, par, ha, hb):
            if a is not None:
                shift(a, par, 0)
                shift(a, par, 1)
                if follows(a):
                    low_keys(a + 1)
                for half in range(2):
                    wait(dve, exped, a, half)
                    wait(dve, inverse, a - 1)
                    nc.vector.tensor_reduce(den[:, HB * half:HB * half + HB], e[par][:, HB * half:HB * half + HB, :],
                                            AX.X, ALU.add).then_inc(summed.sem, 1)
                wait(dve, summed, a, 1)
                wait(dve, prob, a - 1, 1)
                nc.vector.reciprocal(rden[:], den[:]).then_inc(inverse.sem, 1)
            if b is not None:
                if not (isinstance(b, int) and b == 0):
                    add(b - 1)
                keep(b, 0)
                keep(b, 1)
                if a is None:
                    for done in range(NB - 1):
                        if done == 0:
                            wait(dve, added, NB - 2)
                        k.gather(dve, 1, done)
                    add(b)

        low_keys(0)
        pipelined(dve, body, heads=2, peel_last=True)

    def gpsimd(pool):
        prob.start(pool)

        def body(a, b, par, ha, hb):
            if a is None:
                return
            wait(pool, inverse, a)
            for half in range(2):
                tile = e[par][:, HB * half:HB * half + HB, :]
                nc.gpsimd.tensor_tensor(tile, tile, rden[:, HB * half:HB * half + HB].rearrange("q (h o) -> q h o", o=1)
                                        .to_broadcast([SQ, HB, SQ]), ALU.mult).then_inc(prob.sem, 1)

        pipelined(pool, body)

    return Stage(sync=start_loads), Stage(sync=sync, tensor=tensor, scalar=scalar, vector=vector, gpsimd=gpsimd)



def route(k, tag, n_exp, n_group, top_group, top_k, router, bias, fill, tiny, normed, st):
    nc, P = k.nc, k.psum
    E2, SCALE, per = n_exp + 2, 2.5, n_exp // n_group
    def sb(name, shape, dt=F32):
        return k.sbuf(f"r{tag}_{name}", shape, dt, st)

    raw, rH, rL = sb("raw", [128, KT, n_exp]), sb("rH", [128, KT, n_exp], F32R), sb("rL", [128, KT, n_exp], F32R)
    bias_sb = sb("bias", [SQ, n_exp])
    ex, score = sb("ex", [SQ, NB, n_exp]), sb("score", [SQ, NB, n_exp])
    choice = sb("choice", [SQ, NB, n_exp])
    pair = [sb(f"pair{i}", [SQ, NB, n_group, 2]) for i in range(2)]
    two = [sb(f"two{i}", [SQ, NB, n_group]) for i in range(3)]
    gsum, gkeep = sb("gsum", [SQ, NB, n_group]), sb("gkeep", [SQ, NB, n_group])
    glow, gcmp, gcmp2 = sb("glow", [SQ, n_group, n_group]), sb("gcmp", [SQ, NB, n_group, n_group]), sb("gcmp2", [SQ, NB, n_group, n_group])
    masked, top8, rest = sb("masked", [SQ, NB, n_exp]), sb("top8", [SQ, NB, 8]), sb("rest", [SQ, NB, n_exp])
    wsum, wall = sb("wsum", [SQ, NB]), sb("wall", [SQ, NB, E2])
    wT, logT = sb("wT", [E2, T]), sb("logT", [n_exp, T])
    loaded, logit, sig, turned, moved, stored = (k.sem(st, f"r{tag}_{n}") for n in
                                                 ("loaded", "logit", "sig", "turned", "moved", "stored"))
    split, step, weights, logit_t, kept_t = (k.sem(st, f"r{tag}_{n}") for n in ("split", "step", "weights", "logit_t", "kept_t"))
    n_step = [0]

    def sync(sp):
        sp.dma_start(raw[:], router).then_inc(loaded, 16)
        sp.dma_start(bias_sb[:], bias.partition_broadcast(SQ)).then_inc(loaded, 16)
        sp.dma_start(glow[:], k.dram[f"earlier{n_group}"].partition_broadcast(SQ)).then_inc(loaded, 16)

    def store(sp):
        sp.wait_ge(moved, NB // 4)
        sp.dma_start(k.dram["route"][0:E2, :], wT[:]).then_inc(stored, 16)
        sp.wait_ge(stored, 16)

    def tensor(pe):
        pe.wait_ge(*normed)
        pe.wait_ge(split, 2)
        for c in range(NCH):
            n = 0
            for kt in range(KT):
                for x in (k.xnH, k.xnL):
                    for r in (rH, rL):
                        last = nc.tensor.matmul(P[0:n_exp, c, 0:CH], r[:, kt, :], x[:, kt, c * CH:(c + 1) * CH],
                                                start=(n == 0), stop=(n == 7))
                        n += 1
            last.then_inc(logit_t, 1)
        for b in range(NB):
            if b % 4 == 0:
                pe.wait_ge(kept_t, b // 4 + 1)
            last = nc.tensor.transpose(P[0:SQ, 0, b * n_exp:(b + 1) * n_exp], logT[:, b * SQ:(b + 1) * SQ],
                                       k.ident[0:n_exp, 0:n_exp])
        last.then_inc(logit, 1)

    def turn(pe):
        pe.wait_ge(weights, 1)
        for b in range(NB):
            last = nc.tensor.transpose(P[0:E2, b // 4, (b % 4) * SQ:(b % 4 + 1) * SQ], wall[:, b, :],
                                       k.ident[0:SQ, 0:SQ])
            if b % 4 == 3:
                last.then_inc(turned, 1)

    def scalar(act):
        for c in range(NCH):
            act.wait_ge(logit_t, c + 1)
            nc.scalar.copy(logT[:, c * CH:(c + 1) * CH], P[0:n_exp, c, 0:CH]).then_inc(kept_t, 1)
        act.wait_ge(logit, 1)
        nc.scalar.activation(ex[:].rearrange("q b e -> q (b e)"), P[0:SQ, 0, 0:NB * n_exp], ACT.Exp, scale=-1.0
                             ).then_inc(sig, 1)

    def move(act):
        for i in range(NB // 4):
            act.wait_ge(turned, i + 1)
            nc.scalar.copy(wT[:, i * CH:(i + 1) * CH], P[0:E2, i, 0:CH]).then_inc(moved, 1)

    def split_router(dve):
        dve.wait_ge(loaded, 48)
        nc.vector.tensor_copy(rH[:], raw[:]).then_inc(split, 1)
        dve.wait_ge(split, 1)
        nc.vector.tensor_tensor(rL[:], raw[:], rH[:].bitcast(F32), ALU.subtract).then_inc(split, 1)

    def vector(dve):
        def then(ins):
            n_step[0] += 1
            ins.then_inc(step, 1)
            dve.wait_ge(step, n_step[0])

        def rank(values, n, earlier, cmp, cmp2, out):
            shape = [SQ, NB, n, n]
            this = values[:].rearrange("q b (g o) -> q b g o", o=1).to_broadcast(shape)
            other = values[:].rearrange("q b (o g) -> q b o g", o=1).to_broadcast(shape)
            early = earlier[:].rearrange("q (o g) h -> q o g h", o=1).to_broadcast(shape)
            then(nc.vector.tensor_tensor(cmp[:], other, this, ALU.is_equal))
            then(nc.vector.tensor_tensor(cmp[:], cmp[:], early, ALU.mult))
            then(nc.vector.tensor_tensor(cmp2[:], other, this, ALU.is_gt))
            then(nc.vector.tensor_tensor(cmp[:], cmp[:], cmp2[:], ALU.add))
            then(nc.vector.tensor_reduce(out[:], cmp[:], AX.X, ALU.add))

        dve.wait_ge(sig, 1)
        then(nc.vector.tensor_scalar(ex[:], ex[:], 1.0, None, ALU.add))
        then(nc.vector.reciprocal(score[:], ex[:]))
        then(nc.vector.tensor_tensor(choice[:], score[:],
                                     bias_sb[:].rearrange("q (o e) -> q o e", o=1).to_broadcast([SQ, NB, n_exp]), ALU.add))
        quad = choice[:].rearrange("q b (g h e) -> q b g h e", g=n_group, h=2)
        for h in range(2):
            for op, which in ((ALU.max, 0), (ALU.min, 1)):
                then(nc.vector.tensor_tensor(pair[which][:, :, :, h], quad[:, :, :, h, 0], quad[:, :, :, h, 1], op))
        then(nc.vector.tensor_tensor(two[0][:], pair[0][:, :, :, 0], pair[0][:, :, :, 1], ALU.max))
        then(nc.vector.tensor_tensor(two[1][:], pair[0][:, :, :, 0], pair[0][:, :, :, 1], ALU.min))
        then(nc.vector.tensor_tensor(two[2][:], pair[1][:, :, :, 0], pair[1][:, :, :, 1], ALU.max))
        then(nc.vector.tensor_tensor(two[1][:], two[1][:], two[2][:], ALU.max))
        then(nc.vector.tensor_tensor(gsum[:], two[0][:], two[1][:], ALU.add))
        rank(gsum, n_group, glow, gcmp, gcmp2, gkeep)
        then(nc.vector.tensor_scalar(gkeep[:], gkeep[:], float(top_group), None, ALU.is_lt))
        keep4 = gkeep[:].rearrange("q b (g o) -> q b g o", o=1).to_broadcast([SQ, NB, n_group, per])
        then(nc.vector.tensor_tensor(masked[:].rearrange("q b (g e) -> q b g e", g=n_group),
                                     choice[:].rearrange("q b (g e) -> q b g e", g=n_group), keep4, ALU.mult))
        if fill:
            then(nc.vector.tensor_scalar(gkeep[:], gkeep[:], -1.0, -LOWEST, ALU.add, ALU.mult))
            then(nc.vector.tensor_tensor(masked[:].rearrange("q b (g e) -> q b g e", g=n_group),
                                         masked[:].rearrange("q b (g e) -> q b g e", g=n_group), keep4, ALU.add))
        then(nc.vector.tensor_scalar(masked[:], masked[:], 0.0, None, ALU.add))
        for b in range(NB):
            nc.vector.max(top8[:, b, :], masked[:, b, :]).then_inc(step, 1)
        n_step[0] += NB
        dve.wait_ge(step, n_step[0])
        if top_k < 8:
            then(nc.vector.memset(top8[:, :, top_k:8], HIGHEST))
        for b in range(NB):
            nc.vector.match_replace(rest[:, b, :], top8[:, b, :], masked[:, b, :], CHOSEN).then_inc(step, 1)
        n_step[0] += NB
        dve.wait_ge(step, n_step[0])
        then(nc.vector.tensor_scalar(rest[:], rest[:], CHOSEN, None, ALU.is_equal))
        then(nc.vector.tensor_tensor(rest[:], rest[:], score[:], ALU.mult))
        then(nc.vector.tensor_reduce(wsum[:], rest[:], AX.X, ALU.add))
        if tiny:
            then(nc.vector.tensor_scalar(wsum[:], wsum[:], tiny, None, ALU.add))
        then(nc.vector.reciprocal(wsum[:], wsum[:]))
        then(nc.vector.tensor_scalar(wsum[:], wsum[:], SCALE, None, ALU.mult))
        then(nc.vector.memset(wall[:, :, n_exp:E2], 1.0))
        nc.vector.tensor_tensor(wall[:, :, 0:n_exp], rest[:],
                                wsum[:].rearrange("q (b o) -> q b o", o=1).to_broadcast([SQ, NB, n_exp]),
                                ALU.mult).then_inc(weights, 1)
    logits = Stage(sync=sync, tensor=tensor, scalar=scalar, vector=split_router)
    return logits, Stage(vector=vector), Stage(sync=store, tensor=turn, scalar=move)


class Tally:

    AHEAD = 4

    def __init__(self, k, stack, name, unit=1):
        self.sem, self.unit = k.sem(stack, name), unit

    def start(self, eng):
        eng.sem_inc(self.sem, self.AHEAD * self.unit)

    def upto(self, n):
        return (n + self.AHEAD + 1) * self.unit


def until(eng, tally, n):
    eng.wait_ge(tally.sem, tally.upto(n))


def experts(k, tag, n_exp, weights, gate, st):
    nc, P = k.nc, k.psum
    E2, HT = n_exp + 2, T // 2
    GU, NW = 4 * 128, 6 * 128
    def sb(name, shape, dt=F32):
        return k.sbuf(f"m{tag}_{name}", shape, dt, st)

    def tally(name, unit=1):
        return Tally(k, st, f"m{tag}_{name}", unit)

    wraw = [sb(f"wraw{i}", [128, NW]) for i in range(2)]
    wH = [sb(f"wH{i}", [128, NW], F32R) for i in range(2)]
    wL = [sb(f"wL{i}", [128, NW], F32R) for i in range(2)]
    row = [sb(f"row{i}", [1, HT]) for i in range(2)]
    wide = [sb(f"wide{i}", [128, HT]) for i in range(2)]
    sg = [sb(f"sg{i}", [128, CH]) for i in range(2)]
    act_ = [sb(f"act{i}", [128, CH]) for i in range(2)]
    aH = [sb(f"aH{i}", [128, CH], F32R) for i in range(4)]
    aL = [sb(f"aL{i}", [128, CH], F32R) for i in range(4)]
    y = sb("y", [128, KT, 2, CH])
    w_in, row_in = [tally(f"w_in{i}", 16) for i in range(2)], [tally(f"row_in{i}", 16) for i in range(2)]
    gu_high, gu_low, d_high, d_low, spread = (tally(x) for x in ("gu_high", "gu_low", "d_high", "d_low", "spread"))
    gated, upped, silu, weighed, acted, a_high, a_low, downed = (
        tally(x) for x in ("gated", "upped", "silu", "weighed", "acted", "a_high", "a_low", "downed"))
    row_ok = tally("row_ok")
    y_kept, y_turned, added = tally("y_kept"), tally("y_turned"), tally("added")

    def halves(eng, body, tail):
        for half in range(2):
            n0 = half * E2
            body(n0, 0, True)
            body(n0 + 1, 1, None)
            with eng.Fori(1, E2 // 2) as j:
                body(2 * j + n0, 0, False)
                body(2 * j + n0 + 1, 1, False)
            tail(n0 + E2 - 1, half)

    def load_weights(sp, n, j, par):
        until(sp, gu_high, n - 2)
        until(sp, gu_low, n - 2)
        until(sp, d_high, n - 2)
        until(sp, d_low, n - 2)
        sp.dma_start(wraw[par][:], weights[ds(2 * j + par, 1)].rearrange("o p n -> (o p) n")).then_inc(w_in[par].sem, 16)

    def load_row(sp, n, j, par, half):
        until(sp, spread, n - 2)
        sp.dma_start(row[par][:], k.dram["route"][ds(2 * j + par, 1), half * HT:(half + 1) * HT]).then_inc(row_in[par].sem, 16)

    def sync_first(sp):
        for i in range(2):
            w_in[i].start(sp)
            row_in[i].start(sp)
        for par in range(2):
            load_weights(sp, par, 0, par)

    def sync(sp):
        for par in range(2):
            load_row(sp, par, 0, par, 0)
        for half in range(2):
            with sp.Fori(1 - half, E2 // 2) as j:
                for par in range(2):
                    n = 2 * j + (half * E2 + par)
                    load_weights(sp, n, j, par)
                    load_row(sp, n, j, par, half)

    def tensor(pe, first_part=False):
        def project(par, c, half_c, bank, tally_, lo, u):
            for kt in range(KT):
                w = slice(lo + kt * 128, lo + (kt + 1) * 128)
                xH, xL = (x[:, kt, half_c] for x in (k.xnH, k.xnL))
                out = P[:, bank, 0:CH]
                nc.tensor.matmul(out, wH[par][:, w], xH, start=(kt == 0), stop=False)
                nc.tensor.matmul(out, wH[par][:, w], xL, start=False, stop=False)
                last = nc.tensor.matmul(out, wL[par][:, w], xH, start=False, stop=(kt == KT - 1))
            last.then_inc(tally_.sem, 1)

        def down(n, par, c, start, stop):
            u = 2 * n + c
            until(pe, d_high, n)
            until(pe, d_low, n)
            until(pe, a_low, u)
            i = 2 * par + c
            for m in range(KT):
                w = slice(GU + m * 128, GU + (m + 1) * 128)
                out = P[:, 2 * m + c, 0:CH]
                nc.tensor.matmul(out, wH[par][:, w], aH[i][:], start=start, stop=False, skip_group_check=True)
                nc.tensor.matmul(out, wH[par][:, w], aL[i][:], start=False, stop=False, skip_group_check=True)
                last = nc.tensor.matmul(out, wL[par][:, w], aH[i][:], start=False, stop=stop, skip_group_check=True)
            last.then_inc(downed.sem, 1)

        def body(n, par, first):
            if not (isinstance(n, int) and n == 0):
                gates_and_ups(n, par, first)

        def gates_and_ups(n, par, first):
            half = current[0]
            if first is True and half:
                until(pe, added, 3)
            until(pe, gu_high, n)
            until(pe, gu_low, n)
            for c in range(2):
                u = 2 * n + c
                cols = slice(half * HT + c * CH, half * HT + (c + 1) * CH)
                until(pe, silu, u - 2)
                project(par, c, cols, 4 + c, gated, 0, u)
                until(pe, acted, u - 2)
                project(par, c, cols, 6 + c, upped, 2 * 128, u)
                if first is not True:
                    if first is None and c == 0 and half:
                        until(pe, y_kept, half - 1)
                    down(n - 1, 1 - par, c, first is None, False)

        def tail(n, half):
            for c in range(2):
                down(n, 1, c, False, True)
            until(pe, y_kept, half)
            until(pe, acted, 2 * n + 1)
            for i in range(4):
                for s in range(2):
                    tok = (2 * i + s) * SQ
                    for m in range(KT):
                        last = nc.tensor.transpose(P[0:SQ, 4 + i, s * D + m * 128:s * D + (m + 1) * 128],
                                                   y[:, m, tok // CH, tok % CH:tok % CH + SQ], k.ident[:])
                last.then_inc(y_turned.sem, 1)
            current[0] += 1

        current = [0]
        if first_part:
            for t in (gated, upped, downed, y_turned):
                t.start(pe)
            gates_and_ups(0, 0, True)
        else:
            halves(pe, body, tail)

    def scalar_first(act):
        for t in (gu_high, d_high, silu, y_kept):
            t.start(act)
        act.wait_ge(w_in[0].sem, w_in[0].upto(0))
        gate_up_high(0)
        down_high(0)

    def gate_up_high(par):
        nc.scalar.copy(wH[par][:, 0:GU], wraw[par][:, 0:GU]).then_inc(gu_high.sem, 1)

    def down_high(par):
        nc.scalar.copy(wH[par][:, GU:NW], wraw[par][:, GU:NW]).then_inc(d_high.sem, 1)

    def scalar(act):
        def silu_of(u, c):
            until(act, gated, u)
            until(act, acted, u - 2)
            nc.scalar.activation(sg[c][:], P[:, 4 + c, 0:CH], ACT.Silu).then_inc(silu.sem, 1)

        def body(n, par, first):
            if isinstance(n, int) and n == 0:
                silu_of(0, 0)
                return
            act.wait_ge(w_in[par].sem, load_count(n, par, w_in[par]))
            until(act, upped, 2 * n - 3)
            gate_up_high(par)
            if first is not True:
                silu_of(2 * n - 1, 1)
            until(act, downed, 2 * n - 3)
            down_high(par)
            silu_of(2 * n, 0)

        def tail(n, half):
            silu_of(2 * n + 1, 1)
            until(act, downed, 2 * n + 1)
            if half:
                until(act, y_turned, 3)
            nc.scalar.copy(y[:].rearrange("p m c n -> p (m c) n"), P[:, 0:4, 0:CH]).then_inc(y_kept.sem, 1)

        def load_count(n, par, t):
            return t.upto(0) + (n - par) * 8

        halves(act, body, tail)

    def gpsimd(pool):
        spread.start(pool)
        weighed.start(pool)

        def body(n, par, first):
            pool.wait_ge(row_in[par].sem, row_in[par].upto(0) + (n - par) * 8)
            until(pool, weighed, 2 * n - 3)
            pool.sem_inc(row_ok.sem)
            nc.gpsimd.partition_broadcast(wide[par][:], row[par][:]).then_inc(spread.sem, 1)
            until(pool, spread, n)
            for c in range(2):
                until(pool, silu, 2 * n + c)
                nc.gpsimd.tensor_tensor(sg[c][:], sg[c][:], wide[par][:, c * CH:(c + 1) * CH], ALU.mult
                                        ).then_inc(weighed.sem, 1)

        halves(pool, body, lambda n, half: None)

    def vector_first(dve):
        for t in (gu_low, d_low, acted, a_high, a_low, added):
            t.start(dve)
        gate_up_low(dve, 0, 0)
        down_low(dve, 0, 0)

    def gate_up_low(dve, n, par):
        until(dve, gu_high, n)
        nc.vector.tensor_tensor(wL[par][:, 0:GU], wraw[par][:, 0:GU], wH[par][:, 0:GU].bitcast(F32),
                                ALU.subtract).then_inc(gu_low.sem, 1)

    def down_low(dve, n, par):
        until(dve, d_high, n)
        nc.vector.tensor_tensor(wL[par][:, GU:NW], wraw[par][:, GU:NW], wH[par][:, GU:NW].bitcast(F32),
                                ALU.subtract).then_inc(d_low.sem, 1)

    def vector(dve):
        def act_of(n, par, c):
            u, i = 2 * n + c, 2 * par + c
            until(dve, weighed, u)
            until(dve, upped, u)
            until(dve, a_low, u - 2)
            nc.vector.tensor_tensor(act_[c][:], sg[c][:], P[:, 6 + c, 0:CH], ALU.mult).then_inc(acted.sem, 1)
            until(dve, acted, u)
            until(dve, downed, u - 4)
            nc.vector.tensor_copy(aH[i][:], act_[c][:]).then_inc(a_high.sem, 1)
            until(dve, a_high, u)
            nc.vector.tensor_tensor(aL[i][:], act_[c][:], aH[i][:].bitcast(F32), ALU.subtract).then_inc(a_low.sem, 1)

        def body(n, par, first):
            split = not (isinstance(n, int) and n == 0)
            if split:
                gate_up_low(dve, n, par)
            if first is not True:
                act_of(n - 1, 1 - par, 1)
            if split:
                down_low(dve, n, par)
            act_of(n, par, 0)

        def tail(n, half):
            act_of(n, 1, 1)
            for i in range(4):
                until(dve, y_turned, 4 * half + i)
                for s in range(2):
                    b = 8 * half + 2 * i + s
                    last = nc.vector.scalar_tensor_tensor(out=k.x[:, b, :], in0=P[0:SQ, 4 + i, s * D:(s + 1) * D],
                                                          scalar=k.gates[0:SQ, gate:gate + 1], in1=k.x[:, b, :],
                                                          op0=ALU.mult, op1=ALU.add)
                last.then_inc(added.sem, 1)

        halves(dve, body, tail)

    first = Stage(sync=sync_first, tensor=lambda pe: tensor(pe, True), scalar=scalar_first, vector=vector_first)
    return first, Stage(sync=sync, tensor=tensor, scalar=scalar, vector=vector, gpsimd=gpsimd)


def feed_forward(k, tag, n_exp, n_group, top_group, top_k, fill, tiny):
    with ExitStack() as st:
        norm, normed = layer_norm(k, 2 * tag + 1, st)
        logits, choice, spread = route(k, tag, n_exp, n_group, top_group, top_k, k.dram[f"router{tag}"], k.dram[f"bias{tag}"],
                                       fill, tiny, normed, st)
        first, rest = experts(k, tag, n_exp, k.dram[f"experts{tag}"], 2 + tag, st)
        together(k, norm, logits, first, choice, spread, rest)



def prepare_1(k, wa, mm, v1, st):
    nc, P = k.nc, k.psum
    waH, waL = wa
    wqk = k.sbuf("wqk1", [128, NH, D + DCQ], F32, st)
    wvo = k.sbuf("wvo1", [128, NH, DC + D], F32, st)
    wr = k.sbuf("wr1", [DC, NH, DCQ + DC], F32, st)
    in_qk, in_vo, in_r, qk, high, low, vo, vo_kept, rr, rr_kept = (
        k.sem(st, f"p1_{n}") for n in ("in_qk", "in_vo", "in_r", "qk", "high", "low", "vo", "vo_kept", "rr", "rr_kept"))
    def sync(sp):
        sp.dma_start(wqk[:], k.dram["wqk1"]).then_inc(in_qk, 16)
        sp.dma_start(wr[:], k.dram["wr1"]).then_inc(in_r, 16)
        sp.dma_start(wvo[:], k.dram["wvo1"]).then_inc(in_vo, 16)

    def heads(pe, which):
        for h in which:
            if h >= 4:
                pe.wait_ge(low, h - 3)
            for kt in range(KT):
                last = nc.tensor.matmul(P[:, h % 4, kt * DCQ:(kt + 1) * DCQ], wqk[:, h, kt * 128:(kt + 1) * 128],
                                        wqk[:, h, D:], start=True, stop=True)
            last.then_inc(qk, 1)

    def tensor_first(pe):
        pe.wait_ge(in_qk, 16)
        heads(pe, range(4))

    def tensor(pe, banks_free):
        heads(pe, range(4, NH))
        pe.wait_ge(in_r, 16)
        pe.wait_ge(*banks_free)
        for half in range(2):
            if half:
                pe.wait_ge(rr_kept, 1)
            for h in range(NH):
                last = nc.tensor.matmul(P[0:HALF, 6 + h // 8, (h % 8) * DC:(h % 8 + 1) * DC],
                                        wr[:, h, half * HALF:(half + 1) * HALF], wr[:, h, DCQ:], start=True, stop=True)
            last.then_inc(rr, 1)
        pe.wait_ge(in_vo, 16)
        for i in range(NH // 2):
            if i >= 4 and i % 2 == 0:
                pe.wait_ge(vo_kept, i // 2 - 1)
            for up in range(2):
                h = 8 * (i // 4) + i % 4 + 4 * up
                last = nc.tensor.matmul(P[64 * up:64 * up + 64, 4 + i // 2 % 2, (i % 2) * D:(i % 2 + 1) * D],
                                        wvo[:, h, 0:DC], wvo[:, h, DC:], start=True, stop=True)
            if i % 2:
                last.then_inc(vo, 1)

    def of_head(tile, h):
        return tile[:, :, h * DCQ:(h + 1) * DCQ]

    def bank(h):
        return P[:, h % 4, 0:KT * DCQ].rearrange("p (t n) -> p t n", t=KT)

    def high_parts(act, which):
        for h in which:
            act.wait_ge(qk, h + 1)
            nc.scalar.copy(of_head(waH, h), bank(h)).then_inc(high, 1)

    def scalar(act):
        high_parts(act, range(4, NH))
        for i in range(NH // 4):
            act.wait_ge(vo, i + 1)
            nc.scalar.copy(v1[:, 2 * i:2 * i + 2, :].rearrange("p h n -> p (h n)"), P[:, 4 + i % 2, :]).then_inc(vo_kept, 1)

    def low_parts(dve, which):
        for h in which:
            dve.wait_ge(high, h + 1)
            nc.vector.tensor_tensor(of_head(waL, h), bank(h), of_head(waH, h).bitcast(F32), ALU.subtract).then_inc(low, 1)

    def vector(dve):
        low_parts(dve, range(4, NH))
        for half in range(2):
            dve.wait_ge(rr, half + 1)
            nc.vector.tensor_copy(mm[:, half, :], P[0:HALF, 6:8, :].rearrange("p b n -> p (b n)")).then_inc(rr_kept, 1)
    first = Stage(sync=sync, tensor=tensor_first, scalar=lambda act: high_parts(act, range(4)),
                  vector=lambda dve: low_parts(dve, range(4)))
    return first, lambda banks_free: Stage(tensor=lambda pe: tensor(pe, banks_free), scalar=scalar, vector=vector)



def queries_1(k, wa, mm, st):
    nc, P = k.nc, k.psum
    NPR = NH // 2
    rope = k.sbuf("q1_rope", [HALF, 2, 2, SQ], F32, st)
    prods = [[k.sbuf(f"q1_prod{hh}{half}", [HALF, 2, CH], F32, st) for half in range(2)] for hh in range(2)]
    roped = [k.sbuf(f"q1_roped{i}", [HALF, 2, 2, CH], F32, st) for i in range(2)]
    qs = [k.sbuf(f"q1_out{i}", [128, 4, 2, 4, SQ], F32R, st) for i in range(2)]
    rope_in = k.sem(st, "q1_rope_in")
    big, multiplied, added, lat, high, low = (Tally(k, st, f"q1_{n}") for n in ("big", "multiplied", "added", "lat", "high", "low"))
    stored = [Tally(k, st, f"q1_stored{i}", 32) for i in range(2)]

    def chunks(eng, body, tail):
        for p in range(NPR):
            body(0, p, p % 2, p == 0)
        with eng.Fori(1, NCH) as c:
            for p in range(NPR):
                body(c, p, p % 2, False)
        tail()

    def tensor(pe):
        for t in (big, lat):
            t.start(pe)

        def latent(g, par):
            until(pe, added, 4 * g + 3)
            until(pe, low, g - 2)
            for half in range(2):
                for hh in range(2):
                    last = nc.tensor.matmul(P[64 * hh:64 * hh + 64, 4 + par, 0:CH], mm_of(half, pair_done[0] + 8 * hh),
                                            roped[par][:, hh, half, :], start=(half == 0), stop=(half == 1))
            last.then_inc(lat.sem, 1)

        def mm_of(half, h):
            return mm[:, half, h * DC:(h + 1) * DC]

        pair_done = [0]

        def body(c, p, par, first):
            g = NPR * c + p
            for hh in range(2):
                h, i = p + 8 * hh, 2 * g + hh
                until(pe, multiplied, 2 * (i - 2) + 1)
                for half in range(2):
                    w = slice(h * DCQ + half * HALF, h * DCQ + (half + 1) * HALF)
                    out = P[0:HALF, 2 * hh + half, 0:CH]
                    for kt in range(KT):
                        xH, xL = (x[:, kt, ds(c * CH, CH)] for x in (k.xnH, k.xnL))
                        nc.tensor.matmul(out, wa[0][:, kt, w], xH, start=(kt == 0), stop=False)
                        nc.tensor.matmul(out, wa[0][:, kt, w], xL, start=False, stop=False)
                        last = nc.tensor.matmul(out, wa[1][:, kt, w], xH, start=False, stop=(kt == KT - 1))
                last.then_inc(big.sem, 1)
            if not first:
                pair_done[0] = (p - 1) % NPR
                latent(g - 1, 1 - par)

        def tail():
            pair_done[0] = NPR - 1
            latent(NPR * NCH - 1, 1)

        chunks(pe, body, tail)

    def vector(dve):
        for t in (multiplied, low):
            t.start(dve)
        dve.wait_ge(rope_in, 16)

        def low_part(g, p):
            par = p % 2
            until(dve, high, g)
            nc.vector.tensor_tensor(qs[p // 4][:, :, 1, p % 4, :], by_sequence(P[:, 4 + par, 0:CH]),
                                    qs[p // 4][:, :, 0, p % 4, :].bitcast(F32), ALU.subtract
                                    ).then_inc(low.sem, 1)

        def body(c, p, par, first):
            g = NPR * c + p
            for hh in range(2):
                i = 2 * g + hh
                until(dve, big, i)
                until(dve, added, 2 * (i - 2) + 1)
                for half in range(2):
                    nc.vector.tensor_tensor(
                        prods[hh][half][:].rearrange("p t (b q) -> p t b q", b=4),
                        P[0:HALF, 2 * hh + half, 0:CH].rearrange("p (t b q) -> p t b q", t=1, b=4).to_broadcast([HALF, 2, 4, SQ]),
                        rope[:, half].rearrange("p t (o q) -> p t o q", o=1).to_broadcast([HALF, 2, 4, SQ]),
                        ALU.mult).then_inc(multiplied.sem, 1)
            if not first:
                low_part(g - 1, (p - 1) % NPR)

        chunks(dve, body, lambda: low_part(NPR * NCH - 1, NPR - 1))

    def gpsimd(pool):
        added.start(pool)

        def body(c, p, par, first):
            g = NPR * c + p
            for hh in range(2):
                i = 2 * g + hh
                until(pool, multiplied, 2 * i + 1)
                until(pool, lat, g - 2)
                for half, op in ((0, ALU.subtract), (1, ALU.add)):
                    nc.gpsimd.tensor_tensor(roped[par][:, hh, half, :], prods[hh][0][:, half, :], prods[hh][1][:, half, :], op
                                            ).then_inc(added.sem, 1)

        chunks(pool, body, lambda: None)

    def scalar(act):
        high.start(act)

        def body(c, p, par, first):
            g = NPR * c + p
            until(act, lat, g)
            if p % 4 == 0:
                until(act, stored[p // 4], c - 1)
            nc.scalar.copy(qs[p // 4][:, :, 0, p % 4, :], by_sequence(P[:, 4 + par, 0:CH])).then_inc(high.sem, 1)

        chunks(act, body, lambda: None)

    def sync(sp):
        sp.dma_start(rope[:], k.dram["rope_q"]).then_inc(rope_in, 16)
        for t in stored:
            t.start(sp)

        def body(c, p, par, first):
            if p % 4 == 3:
                until(sp, low, NPR * c + p)
                store_queries(k, sp, qs[p // 4], c, p // 4, stored[p // 4].sem)

        def tail():
            for t in stored:
                until(sp, t, NCH - 1)

        chunks(sp, body, tail)

    return Stage(sync=sync, tensor=tensor, scalar=scalar, vector=vector, gpsimd=gpsimd)



class Keys:

    def __init__(self, k, st):
        def sb(name, shape, dt=F32):
            return k.sbuf(f"a1_{name}", shape, dt, st)

        self.k = k
        self.rope = sb("rope", [128, 2, NKT, DC])
        self.ctx = [sb(f"ctx{i}", [128, NKT, DC]) for i in range(2)]
        self.byc, self.bys = sb("byc", [128, NKT, DC]), sb("bys", [128, NKT, DC])
        self.kv = [sb(f"kv{i}", [128, NKT, DC]) for i in range(2)]
        self.kv2 = sb("kv2", [128, NKT, 2 * DC])
        self.cleared, self.rope_in = k.sem(st, "a1_cleared"), k.sem(st, "a1_rope_in")
        self.ctx_in = [Count(k, st, f"a1_ctx_in{i}", 1, 32) for i in range(2)]
        self.times_cs, self.roped, self.roped2 = (Count(k, st, f"a1_{n}", per) for n, per in
                                                  (("times_cs", 3), ("roped", 1), ("roped2", 2)))

    def load_ctx(self, sp, a, par):
        k, ctx = self.k, self.ctx
        wait(sp, self.times_cs, a - 2, 2)
        src = k.dram["ctx"][ds(a, 1)].rearrange("o s d -> (o s) d")
        sp.dma_start(ctx[par][:, 0:NKT - 1, :], src[0:128 * (NKT - 1)].rearrange("(t p) d -> p t d", p=128)
                     ).then_inc(self.ctx_in[par].sem, 16)
        sp.dma_start(ctx[par][0:KREST, NKT - 1, :], src[128 * (NKT - 1):SK]).then_inc(self.ctx_in[par].sem, 16)

    def products(self, pool, a, par, ha):
        nc, rope, ctx = self.k.nc, self.rope, self.ctx
        wait(pool, self.ctx_in[par], ha)
        wait(pool, self.roped, a - 1)
        nc.gpsimd.tensor_tensor(self.byc[:], ctx[par][:], rope[:, 0], ALU.mult).then_inc(self.times_cs.sem, 1)
        for i in range(2):
            here, there = slice(32 * i, 32 * i + 32), slice(32 - 32 * i, 64 - 32 * i)
            nc.gpsimd.tensor_tensor(self.bys[:, :, here], ctx[par][:, :, there], rope[:, 1, :, here], ALU.mult
                                    ).then_inc(self.times_cs.sem, 1)

    def sums(self, pool, a, par, kv2_free=None, kv_free=None):
        nc = self.k.nc
        wait(pool, self.times_cs, a, 2)
        if kv2_free:
            wait(pool, *kv2_free)
        for i in range(2):
            nc.gpsimd.tensor_tensor(self.kv2[:, :, i * DC:(i + 1) * DC], self.byc[:], self.bys[:], ALU.add
                                    ).then_inc(self.roped2.sem, 1)
        if kv_free:
            wait(pool, *kv_free)
        nc.gpsimd.tensor_tensor(self.kv[par][:], self.byc[:], self.bys[:], ALU.add).then_inc(self.roped.sem, 1)

    def first_sequence(self):
        def sync(sp):
            for c in self.ctx_in:
                c.start(sp)
            sp.dma_start(self.rope[:], self.k.dram["rope_k"]).then_inc(self.rope_in, 16)
            sp.wait_ge(self.cleared, 1)
            self.load_ctx(sp, 0, 0)

        def clear(pool):
            for c in (self.times_cs, self.roped, self.roped2):
                c.start(pool)
            for i in range(2):
                self.k.nc.gpsimd.memset(self.ctx[i][:, NKT - 1, :], 0.0)
            self.k.nc.gpsimd.drain().then_inc(self.cleared, 1)

        def add(pool):
            pool.wait_ge(self.rope_in, 16)
            self.products(pool, 0, 0, 0)
            self.sums(pool, 0, 0)

        return Stage(sync=sync, gpsimd=clear), Stage(gpsimd=add)


def attention_1(k, v1, keys, spare):
    nc, P = k.nc, k.psum
    NT = (HQ + 127) // 128
    PARTS, UB = 3, 4
    PK = 2 * ((SK + 2 * PARTS - 1) // (2 * PARTS))
    NU, NSLOT, NPAIR = PARTS * NT, NCH * NKT, NCH * NKT // 2
    PRE = 4
    CHAIN_STEPS = 16
    CHAIN, TURN_SHIFT = 38, 8
    unit_slots = {}
    for i in range(NU):
        unit_slots.setdefault(1 - PRE + i * (CHAIN + PRE - 1) // NU, []).append(i)

    def key_rows(t):
        return 128 if t < NKT - 1 else KREST

    with ExitStack() as st:
        def sb(name, shape, dt=F32):
            return k.sbuf(f"a1_{name}", shape, dt, st)

        def count(name, per, unit=1):
            return Count(k, st, f"a1_{name}", per, unit)

        kv, kv2, roped, roped2 = keys.kv, keys.kv2, keys.roped, keys.roped2
        kHH = [spare[0][:, i, 0:SK] for i in range(2)]
        kL = [spare[1][0:DC + 2, i, 0:SK] for i in range(2)]
        qA = [sb(f"qA{i}", [128, HQ], F32R) for i in range(2)]
        qH = [sb(f"qH{i}", [DC + 2, HQ], F32R) for i in range(2)]
        nmax, den = sb("nmax", [128, NT, PARTS]), sb("den", [128, NT, PARTS])
        nm, gap, egap = sb("nm", [128, NT]), sb("gap", [128, NT, PARTS]), sb("egap", [128, NT, PARTS])
        total, shift, shs = sb("total", [128, NT]), sb("shift", [128, NT]), sb("shs", [128, 2, NT], F32R)
        log0, part, delta, series = (sb(n, [128, NT]) for n in ("log0", "part", "delta", "series"))
        rows = sb("rows", [2 * NT, 128])
        pt = [sb(f"pt{i}", [128, 2, CH]) for i in range(3)]
        cc = sb("cc", [128, HQ // 2])

        ones_set = k.sem(st, "a1_ones_set")
        q_in = [[count(f"q_in{i}{c}", 1, 32) for c in range(NCH)] for i in range(2)]
        shift_in = [count(f"shift_in{i}", 1, 16) for i in range(2)]
        shift_out = [count(f"shift_out{i}", 1, 16) for i in range(2)]
        kturn, khigh, klow = count("kturn", 2), count("khigh", 2), count("klow", 2)
        unit, umax, uexp = count("unit", NU), count("umax", NU), count("uexp", NU)
        chain_v, chain_a = count("chain_v", CHAIN_STEPS), count("chain_a", 2)
        sturn, srow = count("sturn", 1), count("srow", 1)
        scored, exped, pair = count("scored", NSLOT), count("exped", NSLOT), count("pair", NPAIR)
        cc_ready, proj, added = count("cc_ready", NCH // 2), count("proj", 1), count("added", 1)

        def key_banks(i):
            return P[:, 2 * i:2 * i + 2, :].rearrange("p b n -> p (b n)")

        SHIFT_BANK = UB - 1

        def unit_rows(i):
            return min(128, HQ - 128 * (i // PARTS))

        def unit_keys(i):
            return i % PARTS * PK, min(PK, SK - i % PARTS * PK)

        def unit_tile(i):
            return P[0:unit_rows(i), i % UB, 0:unit_keys(i)[1]]

        def of_unit(tile, i):
            return tile[0:unit_rows(i), i // PARTS, i % PARTS:i % PARTS + 1]

        def out_bank(par_b, i):
            return 6 + (3 * par_b + i) % 2

        def slot_work(s):
            return 2 * (s // (2 * NKT)) + s % 2, s % (2 * NKT) // 2

        with nc.Block() as block:
            @block.sync
            def _(sp):
                for c in q_in[0] + q_in[1] + shift_in + shift_out:
                    c.start(sp)

                def load_q(a, par, c):
                    wait(sp, scored, a - 2, 2 * NKT * (c // 2 + 1) - 2 + c % 2)
                    src = k.dram["q_lat"][ds(a, 1), :, :, 4 * c:4 * c + 4, :]
                    sp.dma_start(qA[par][:, c * CH:(c + 1) * CH].bitcast(F32), src.rearrange("o l d h q -> (o l d) (h q)")
                                 ).then_inc(q_in[par][c].sem, 16)
                    sp.dma_start(qH[par][0:DC, c * CH:(c + 1) * CH].bitcast(F32), src[:, 0].rearrange("o d h q -> (o d) (h q)")
                                 ).then_inc(q_in[par][c].sem, 16)

                def spread_shift(a, par, ha):
                    wait(sp, srow, a)
                    sp.dma_start(k.dram["shift"][par].rearrange("l (t n) -> (l t) n", n=128), rows[:]
                                 ).then_inc(shift_out[par].sem, 16)
                    wait(sp, shift_out[par], ha)
                    sp.dma_start(qH[par][DC:DC + 2, :].bitcast(F32), k.dram["shift"][par, :, 0:HQ]).then_inc(shift_in[par].sem, 16)

                for c in range(NCH):
                    load_q(0, 0, c)

                def body(a, b, par, ha, hb):
                    if a is None:
                        return
                    more = not (isinstance(a, int) and a == NB - 1)
                    if more:
                        keys.load_ctx(sp, a + 1, 1 - par)
                        for c in range(NCH // 2):
                            load_q(a + 1, 1 - par, c)
                    spread_shift(a, par, ha)
                    if more:
                        for c in range(NCH // 2, NCH):
                            load_q(a + 1, 1 - par, c)

                pipelined(sp, body)

            @block.gpsimd
            def _(pool):
                def body(a, b, par, ha, hb):
                    if a is None:
                        return
                    if not (isinstance(a, int) and a == 0):
                        keys.sums(pool, a, par, (kturn, a - 1, 1), (pair, a - 2, NPAIR - 1))
                    if not (isinstance(a, int) and a == NB - 1):
                        keys.products(pool, a + 1, 1 - par, ha + par)

                pipelined(pool, body)

            @block.tensor
            def _(pe):
                for c in (kturn, unit, sturn, scored, pair, proj):
                    c.start(pe)
                pe.wait_ge(ones_set, 1)

                def turn_keys(a, par, i):
                    if i == 0:
                        wait(pe, roped2, a, 1)
                        wait(pe, uexp, a - 1, NU - 1)
                    else:
                        wait(pe, srow, a - 1)
                    for j in range(6):
                        t = 6 * i + j
                        m = key_rows(t)
                        last = nc.tensor.transpose(key_banks(i)[:, j * 128:j * 128 + m],
                                                   kv2[0:m, t, :], k.ident[0:m, 0:m])
                    last.then_inc(kturn.sem, 1)

                def score_unit(a, par, ha, i):
                    t, m, n0 = i // PARTS, unit_rows(i), 128 * (i // PARTS)
                    first, n = unit_keys(i)
                    if i % PARTS == 0:
                        for c in range(NCH):
                            if (t == 0 and c == 0) or (t and (n0 - 1) // CH < c <= (n0 + m - 1) // CH):
                                wait(pe, q_in[par][c], ha)
                    if i < UB:
                        wait(pe, klow, a, 1)
                    else:
                        wait(pe, uexp, a, i - UB)
                    nc.tensor.matmul(unit_tile(i), qA[par][:, n0:n0 + m], kHH[par][:, first:first + n], start=True, stop=False)
                    nc.tensor.matmul(unit_tile(i), qH[par][0:DC, n0:n0 + m], kL[par][0:DC, first:first + n],
                                     start=False, stop=True).then_inc(unit.sem, 1)

                def turn_shift(a, par):
                    wait(pe, chain_v, a, CHAIN_STEPS - 1)
                    nc.tensor.transpose(P[0:2 * NT, SHIFT_BANK, 0:128], shs[:].rearrange("p l t -> p (l t)").bitcast(F32),
                                        k.ident[:]).then_inc(sturn.sem, 1)

                def scores_t(b, par, hb, s):
                    c, t = slot_work(s)
                    m = key_rows(t)
                    if s == 0:
                        wait(pe, shift_in[par], hb)
                        wait(pe, roped, b)
                    if s < 2:
                        wait(pe, exped, b - 1, s + NSLOT - 2)
                    else:
                        wait(pe, exped, b, s - 2)
                    out, cols, keys = P[0:m, 4 + s % 2, 0:CH], slice(c * CH, (c + 1) * CH), slice(t * 128, t * 128 + m)
                    nc.tensor.matmul(out, kHH[par][:, keys], qA[par][:, cols], start=True, stop=False)
                    nc.tensor.matmul(out, kL[par][:, keys], qH[par][:, cols], start=False, stop=True).then_inc(scored.sem, 1)

                def times_kv(b, par, j):
                    i, t = j // NKT, j % NKT
                    wait(pe, exped, b, 2 * j + 1)
                    if t == 0:
                        if i == 0:
                            wait(pe, cc_ready, b - 1, 1)
                        else:
                            wait(pe, added, b - 1)
                    for up in range(2):
                        last = nc.tensor.matmul(P[64 * up:64 * up + 64, out_bank(par, i), 0:CH], kv[par][:, t, :],
                                                pt[j % 3][:, up, :], start=(t == 0), stop=(t == NKT - 1))
                    last.then_inc(pair.sem, 1)

                def project(b, par, part=None):
                    pairs = range(NH // 2) if part is None else range(2 * part, 2 * part + 2)
                    if pairs[0] == 0:
                        wait(pe, cc_ready, b, 1)
                    for h in pairs:
                        last = nc.tensor.matmul(P[0:SQ, out_bank(par, 2), 0:D], cc[:, h * SQ:(h + 1) * SQ], v1[:, h, :],
                                                start=(h == 0), stop=(h == NH // 2 - 1))
                    if pairs[-1] == NH // 2 - 1:
                        last.then_inc(proj.sem, 1)

                def body(a, b, par, ha, hb):
                    if a is not None:
                        turn_keys(a, par, 0)
                        turn_keys(a, par, 1)
                    for s in range(-PRE, NSLOT):
                        if s < 0 and b is not None and not (isinstance(b, int) and b == 0):
                            project(b - 1, par, s + PRE)
                        if s >= 0 and b is not None:
                            scores_t(b, 1 - par, hb, s)
                        if a is not None:
                            for i in unit_slots.get(s, []):
                                score_unit(a, par, ha, i)
                            if s == CHAIN + TURN_SHIFT:
                                turn_shift(a, par)
                        if b is not None:
                            if s >= 3 and s % 2:
                                times_kv(b, 1 - par, (s - 3) // 2)
                    if b is not None:
                        times_kv(b, 1 - par, NPAIR - 1)
                        if a is None:
                            project(b, 1 - par)

                pipelined(pe, body, heads=2)

            @block.scalar
            def _(act):
                for c in (khigh, uexp, chain_a, exped):
                    c.start(act)

                def high_keys(a, par, i):
                    n = 128 * 5 + key_rows(6 * i + 5)
                    wait(act, kturn, a, i)
                    wait(act, scored, a - 2, NSLOT - 1)
                    nc.scalar.copy(kHH[par][:, 768 * i:768 * i + n], key_banks(i)[:, 0:n]).then_inc(khigh.sem, 1)

                def exp_unit(a, par, i):
                    wait(act, umax, a, i)
                    if i == 0:
                        wait(act, chain_v, a - 1, CHAIN_STEPS - 1)
                    nc.scalar.activation(unit_tile(i), unit_tile(i), ACT.Exp, bias=of_unit(nmax, i),
                                         accum_out=of_unit(den, i)).then_inc(uexp.sem, 1)

                def exp_slot(b, s):
                    j, m = s // 2, key_rows(slot_work(s)[1])
                    wait(act, scored, b, s)
                    if s % 2 == 0:
                        if j < 3:
                            wait(act, pair, b - 1, j - 3 + NPAIR)
                        else:
                            wait(act, pair, b, j - 3)
                    nc.scalar.activation(pt[j % 3][0:m, s % 2, :], P[0:m, 4 + s % 2, 0:CH], ACT.Exp).then_inc(exped.sem, 1)

                def body(a, b, par, ha, hb):
                    if a is not None:
                        high_keys(a, par, 0)
                        high_keys(a, par, 1)
                    for s in range(-PRE, NSLOT):
                        if s >= 0 and b is not None:
                            exp_slot(b, s)
                        if a is not None:
                            for i in unit_slots.get(s - 1, []):
                                exp_unit(a, par, i)
                            if s == CHAIN + 1:
                                wait(act, chain_v, a, 1)
                                nc.scalar.activation(egap[:], gap[:], ACT.Exp).then_inc(chain_a.sem, 1)
                            if s == CHAIN + 3:
                                wait(act, chain_v, a, 5)
                                nc.scalar.activation(part[:], log0[:], ACT.Exp, scale=-1.0).then_inc(chain_a.sem, 1)

                pipelined(act, body, heads=2)

            @block.vector
            def _(dve):
                for c in (klow, umax, chain_v, srow, cc_ready, added):
                    c.start(dve)
                for i in range(2):
                    nc.vector.memset(kL[i][DC:DC + 2, :].bitcast(F32), 1.0)
                nc.vector.memset(nmax[:], 0.0)
                nc.vector.memset(den[:], 1.0)
                nc.vector.drain().then_inc(ones_set, 1)
                dve.wait_ge(ones_set, 1)

                def low_keys(a, par, i):
                    n = 128 * 5 + key_rows(6 * i + 5)
                    wait(dve, khigh, a, i)
                    nc.vector.tensor_tensor(kL[par][0:DC, 768 * i:768 * i + n], key_banks(i)[0:DC, 0:n],
                                            kHH[par][0:DC, 768 * i:768 * i + n].bitcast(F32), ALU.subtract).then_inc(klow.sem, 1)

                def max_unit(a, par, i):
                    wait(dve, unit, a, i)
                    if i == 0:
                        wait(dve, chain_v, a - 1, CHAIN_STEPS - 1)
                        wait(dve, uexp, a - 1, NU - 1)
                    nc.vector.tensor_reduce(of_unit(nmax, i), unit_tile(i), AX.X, ALU.max, negate=True).then_inc(umax.sem, 1)

                def every(tile):
                    return tile[:].rearrange("p (t o) -> p t o", o=1).to_broadcast([128, NT, PARTS])

                def chain_1(a):
                    wait(dve, umax, a, NU - 1)
                    wait(dve, chain_v, a - 1, CHAIN_STEPS - 1)
                    nc.vector.tensor_reduce(nm[:], nmax[:], AX.X, ALU.min).then_inc(chain_v.sem, 1)
                    wait(dve, chain_v, a, 0)
                    nc.vector.tensor_tensor(gap[:], every(nm), nmax[:], ALU.subtract).then_inc(chain_v.sem, 1)

                def link(a, i, ins):
                    ins.then_inc(chain_v.sem, 1)
                    wait(dve, chain_v, a, i)

                def chain_2(a):
                    wait(dve, chain_a, a, 0)
                    wait(dve, uexp, a, NU - 1)
                    link(a, 2, nc.vector.tensor_tensor(egap[:], egap[:], den[:], ALU.mult))
                    link(a, 3, nc.vector.tensor_reduce(total[:], egap[:], AX.X, ALU.add))
                    link(a, 4, nc.vector.tensor_copy(log0[:], total[:].bitcast(mybir.dt.int32)))
                    link(a, 5, nc.vector.tensor_scalar(log0[:], log0[:], LN2 / 2 ** 23, -(127 - 0.043) * LN2, ALU.mult, ALU.add))
                    link(a, 6, nc.vector.tensor_tensor(shift[:], nm[:], log0[:], ALU.subtract))

                def chain_3(a):
                    wait(dve, chain_a, a, 1)
                    link(a, 7, nc.vector.tensor_tensor(delta[:], total[:], part[:], ALU.mult))
                    link(a, 8, nc.vector.tensor_scalar(delta[:], delta[:], -1.0, None, ALU.add))
                    link(a, 9, nc.vector.tensor_scalar(series[:], delta[:], -0.25, None, ALU.mult))
                    for i, c in ((10, 1 / 3), (11, -0.5), (12, 1.0)):
                        link(a, i, nc.vector.scalar_tensor_tensor(out=series[:], in0=series[:], scalar=c, in1=delta[:],
                                                                  op0=ALU.add, op1=ALU.mult))
                    link(a, 13, nc.vector.tensor_tensor(shift[:], shift[:], series[:], ALU.subtract))
                    wait(dve, sturn, a - 1)
                    link(a, 14, nc.vector.tensor_copy(shs[:, 0, :], shift[:]))
                    nc.vector.tensor_tensor(shs[:, 1, :], shift[:], shs[:, 0, :].bitcast(F32), ALU.subtract).then_inc(chain_v.sem, 1)

                def row_of_shift(a, par, ha):
                    wait(dve, sturn, a)
                    if not (isinstance(a, int) and a == 0):
                        wait(dve, shift_out[1 - par], ha - 1 + par)
                    nc.vector.tensor_copy(rows[:], P[0:2 * NT, SHIFT_BANK, 0:128]).then_inc(srow.sem, 1)

                def keep(b, par, i):
                    wait(dve, pair, b, (i + 1) * NKT - 1)
                    wait(dve, proj, b - 1)
                    nc.vector.tensor_copy(cc[:, i * CH:(i + 1) * CH], P[:, out_bank(par, i), 0:CH]).then_inc(cc_ready.sem, 1)

                def add(b, par):
                    wait(dve, proj, b)
                    xb = k.x[:, ds(b, 1), :].rearrange("q o d -> q (o d)")
                    nc.vector.scalar_tensor_tensor(out=xb, in0=P[0:SQ, out_bank(par, 2), 0:D], scalar=k.gates[0:SQ, 1:2], in1=xb,
                                                   op0=ALU.mult, op1=ALU.add).then_inc(added.sem, 1)

                def body(a, b, par, ha, hb):
                    if a is not None:
                        low_keys(a, par, 0)
                        low_keys(a, par, 1)
                    for s in range(-PRE, NSLOT):
                        if s == 0 and b is not None and not (isinstance(b, int) and b == 0):
                            add(b - 1, par)
                        if a is not None:
                            for i in unit_slots.get(s, []):
                                max_unit(a, par, i)
                            for n, step in ((0, chain_1), (2, chain_2), (4, chain_3)):
                                if s == CHAIN + n:
                                    step(a)
                            if s == CHAIN + TURN_SHIFT + 1:
                                row_of_shift(a, par, ha)
                        if b is not None:
                            if s == 2 * NKT + 3:
                                keep(b, 1 - par, 0)
                            if s == 1 and a is None:
                                wait(dve, added, NB - 2)
                                for done in range(NB - 1):
                                    k.gather(dve, 3, done)
                    if b is not None:
                        keep(b, 1 - par, 1)
                        if a is None:
                            add(b, 1 - par)

                pipelined(dve, body, heads=2)


def layer_1(k):
    with ExitStack() as st:
        v1 = k.sbuf("v1", [128, NH // 2, D], F32, st)
        wa = [k.sbuf(f"wb{x}", [128, KT, NH * DCQ], F32R, st) for x in "HL"]
        mm = k.sbuf("mm", [HALF, 2, NH * DC], F32, st)
        with ExitStack() as scratch:
            first, prepare = prepare_1(k, wa, mm, v1, scratch)
            norm, banks_free = layer_norm(k, 2, scratch, between_dve=first.vector, between_act=first.scalar, bank0=4)
            together(k, Stage(sync=first.sync, tensor=first.tensor), norm, prepare(banks_free))
        keys = Keys(k, st)
        with ExitStack() as scratch:
            before, after = keys.first_sequence()
            together(k, before, queries_1(k, wa, mm, scratch), after)
        attention_1(k, v1, keys, wa)



def build(nc, dram, stop=99):
    with ExitStack() as stack:
        k = Core(nc, dram, stack)
        with ExitStack() as st:
            wa = [k.sbuf(f"wa{x}", [128, KT, NH * DC], F32R, st) for x in "HL"]
            v0 = k.sbuf("v0", [128, NH // 2, D], F32, st)
            maskq = k.sbuf("maskq", [SQ, SQ], BF16, st)
            identb = k.sbuf("identb", [128, 128], BF16, st)
            with ExitStack() as inner:
                prepare, on_act, on_dve, x_loaded, low_done = prepare_0(k, wa, v0, maskq, identb, inner)
                norm, _ = layer_norm(k, 0, inner, ready=x_loaded, free=low_done, between_dve=on_dve, between_act=on_act)
                together(k, prepare, norm)
            if stop >= 2:
                with ExitStack() as inner:
                    first_stores, queries, chunks_stored = queries_0(k, wa, inner)
                    first_loads, attention = attention_0(k, v0, maskq, identb, chunks_stored, inner)
                    together(k, first_stores, first_loads, queries, attention)
        if stop >= 4:
            feed_forward(k, 0, 32, 8, 4, 8, False, 0.0)
            k.clear_semaphores()
        if stop >= 5:
            layer_1(k)
        if stop >= 6:
            feed_forward(k, 1, 16, 4, 2, 4, True, 1e-20)
        with nc.semaphore("out_stored") as stored, nc.Block() as block:
            @block.sync
            def _(sp):
                sp.dma_start(dram["out"].rearrange("b q d -> q b d"), k.x[:]).then_inc(stored, 16)
                sp.wait_ge(stored, 16)


def lay_out(v):
    f = {n: np.asarray(a) for n, a in v.items()}

    def heads(w):
        return w.reshape(NH, -1, w.shape[-1]).transpose(1, 0, 2)

    def tiles(w):
        return w.reshape(KT, 128, -1).transpose(1, 0, 2).reshape(128, -1)

    def packed(gate, up, down, sg, su, sd):
        rows = [np.concatenate([tiles(g), tiles(u), d], 1) for g, u, d in zip(gate, up, down)]
        for i in range(2):
            c = slice(i * FF, (i + 1) * FF)
            rows.append(np.concatenate([tiles(sg[:, c]), tiles(su[:, c]), sd[c]], 1))
        return np.stack(rows)

    kv = f["L0_xattn_Wkv_expand"]
    out = {
        "x": f["x"], "ctx": f["ctx_512"], "g_xattn": f["g_xattn"], "g_ffn": f["g_ffn"],
        "w_attn0": np.concatenate([heads(f["L0_xattn_Wq"]), heads(kv[:D]), heads(kv[D:]), heads(f["L0_xattn_Wout"].T)], 2),
        "router0": f["L0_ffn_router_w"].reshape(KT, 128, 32).transpose(1, 0, 2), "bias0": f["L0_ffn_router_bias"],
        "experts0": packed(*(f["L0_ffn_" + n] for n in ("w_gate", "w_up", "w_down", "sw_gate", "sw_up", "sw_down"))),
        "wqk1": np.concatenate([f["L1_xattn_Wq"].reshape(NH, 128, D).transpose(1, 0, 2),
                                f["L1_xattn_w_kc_q"].transpose(1, 0, 2)], 2),
        "wvo1": np.concatenate([f["L1_xattn_w_kc_kv"].transpose(1, 0, 2),
                                f["L1_xattn_Wo"].T.reshape(NH, 128, D).transpose(1, 0, 2)], 2),
        "wr1": np.concatenate([f["L1_xattn_W_qr"].transpose(2, 0, 1), f["L1_xattn_W_kr"].transpose(2, 0, 1)], 2),
        "router1": f["L1_ffn_gate_weight"].T.reshape(KT, 128, 16).transpose(1, 0, 2),
        "bias1": f["L1_ffn_e_score_correction_bias"],
        "experts1": packed(*(f["L1_ffn_" + n].swapaxes(-1, -2) for n in ("gate_w", "up_w", "down_w")),
                           *(f["L1_ffn_" + n].T for n in ("sh_gate_w", "sh_up_w", "sh_down_w"))),
        "ident": np.eye(128, dtype=np.float32), "ident_bf16": np.eye(128).astype(mybir.dt.np(BF16)),
        "mask": np.where(np.tril(np.ones((SQ, SQ), bool)), 0, LOWEST).astype(mybir.dt.np(BF16)),
    }
    for n in (8, 4):
        out[f"earlier{n}"] = np.tril(np.ones((n, n), np.float32), -1)

    def rope(length, width):
        inv = np.float32(1.0) / np.float32(10000.0) ** (np.arange(0, width, 2, dtype=np.float32) / np.float32(width))
        angle = np.arange(length, dtype=np.float32)[:, None] * inv[None, :]
        return np.repeat(np.cos(angle), 2, -1), np.repeat(np.sin(angle), 2, -1)

    cos, sin = (t.T.reshape(2, HALF, SQ) for t in rope(SQ, DCQ))
    out["rope_q"] = np.stack([np.stack([cos[0], sin[1]], 1), np.stack([sin[0], cos[1]], 1)], 1)
    cos, sin = (np.pad(t, ((0, NKT * 128 - SK), (0, 0))).reshape(NKT, 128, DC).transpose(1, 0, 2) for t in rope(SK, DC))
    half = np.where(np.arange(DC) < DC // 2, np.float32(-1), np.float32(1))
    out["rope_k"] = np.stack([cos, sin * half], 1)
    return {n: np.ascontiguousarray(a) for n, a in out.items()}


def kernel(**inputs):
    import concourse.bacc as bacc
    from concourse.bass_utils import run_bass_kernel_spmd

    arrays = lay_out(inputs)
    nc = bacc.Bacc("TRN2", target_bir_lowering=False, num_devices=1)
    dram = {n: nc.dram_tensor("in_" + n, a.shape, mybir.dt.from_np(a.dtype), kind="ExternalInput").ap() for n, a in arrays.items()}
    dram["out"] = nc.dram_tensor("out", [NB, SQ, D], F32, kind="ExternalOutput").ap()
    dram["q_lat"] = nc.dram_tensor("q_lat", [NB, 2, DC, NH, SQ], F32).ap()
    dram["shift"] = nc.dram_tensor("shift", [2, 2, 13 * 128], F32).ap()
    dram["route"] = nc.dram_tensor("route", [34, T], F32).ap()
    build(nc, dram)
    result = run_bass_kernel_spmd(nc, [{"in_" + n: a for n, a in arrays.items()}], core_ids=[0])
    return result.results[0]["out"]
```
